# Optimizing a Trainium2 kernel written in Bass

```python
import numpy as np
import jax
import jax.numpy as jnp

def _softmax(x, axis=-1):
    return jax.nn.softmax(x, axis=axis)

def _gelu(x):
    return jax.nn.gelu(x, approximate=True)

def _silu(x):
    return jax.nn.silu(x)

def _sigmoid(x):
    return jax.nn.sigmoid(x)

def _layernorm(x, axis=-1, eps=1e-05):
    m = jnp.mean(x, axis=axis, keepdims=True)
    v = jnp.var(x, axis=axis, keepdims=True)
    return (x - m) / jnp.sqrt(v + eps)

def _scatter_add(tgt, idx, src, axis=0):
    return tgt.at[idx].add(src)

def _segment_sum(src, seg, n):
    return jax.ops.segment_sum(src, seg, n)
kernel_name = 'mk_gnn_resnorm_d2_gnn_r8_68098b'

def setup_inputs(seed: int=0):
    np.random.seed(seed)
    _w = jnp.asarray

    def _rec_inputs():
        import jax
        import jax.numpy as jnp
        _gk = jax.random.key(seed)
        x = -8.776e-05 + 1 * jax.random.normal(jax.random.fold_in(_gk, 1), (6250, 512), jnp.float32)
        src = jax.random.randint(jax.random.fold_in(_gk, 2), (100000,), 0, 6250, jnp.int32)
        dst = jnp.minimum((6250 * jax.random.uniform(jax.random.fold_in(_gk, 3), (100000,)) ** 2.0).astype(jnp.int32), 49999)
        _o = jnp.argsort(dst, stable=True)
        src = src[_o]
        dst = dst[_o]
        return (x, src, dst)
    x, src, dst = _rec_inputs()

    def _L0_gnn_setup():
        import jax, jax.numpy as jnp
        import numpy as np

        def _gcn_conv(x, edge_index, W, b):
            N = x.shape[0]
            loops = jnp.arange(N, dtype=edge_index.dtype)
            src = jnp.concatenate([edge_index[0], loops])
            dst = jnp.concatenate([edge_index[1], loops])
            deg = jax.ops.segment_sum(jnp.ones_like(dst, dtype=x.dtype), dst, num_segments=N)
            dinv = jnp.where(deg > 0, jax.lax.rsqrt(deg), 0.0)
            norm = dinv[src] * dinv[dst]
            xw = x @ W
            msgs = norm[:, None] * xw[src]
            out = jax.ops.segment_sum(msgs, dst, num_segments=N)
            return out + b
        key = jax.random.key(seed)
        ks = jax.random.split(key, 8)
        N, E = (1250, 20000)
        IN, OUT, TC = (512, 512, 256)
        x = jax.random.normal(ks[0], (N, IN), dtype=jnp.float32)
        t_emb = jax.random.normal(ks[1], (TC,), dtype=jnp.float32)
        edge_index = jax.random.randint(ks[2], (2, E), 0, N, dtype=jnp.int64)
        W = jax.random.normal(ks[3], (IN, OUT), dtype=jnp.float32) / np.sqrt(IN)
        b = jnp.zeros((OUT,), dtype=jnp.float32)
        Wt = jax.random.normal(ks[4], (TC, OUT), dtype=jnp.float32) / np.sqrt(TC)
        bt = jnp.zeros((OUT,), dtype=jnp.float32)
        return {'x': x, 't_emb': t_emb, 'edge_index': edge_index, 'W': W, 'b': b, 'Wt': Wt, 'bt': bt}
    _L0_gnn_all = _L0_gnn_setup()
    _L0_gnn_in = {k: v for k, v in _L0_gnn_all.items() if k in ('t_emb', 'W', 'b', 'Wt', 'bt')}
    del _L0_gnn_all

    def _L1_gnn_setup():
        import jax, jax.numpy as jnp
        import numpy as np
        N_NODES = 6250
        N_EDGES = 100000
        D_IN = 512
        D_OUT = 512

        def sage_conv(x, src, dst, Wl, Wr, b, num_nodes):
            msg = x[src]
            summed = jax.ops.segment_sum(msg, dst, num_segments=num_nodes)
            cnt = jax.ops.segment_sum(jnp.ones((src.shape[0],), dtype=x.dtype), dst, num_segments=num_nodes)
            mean = summed / jnp.maximum(cnt, 1.0)[:, None]
            return mean @ Wl.T + x @ Wr.T + b
        key = jax.random.key(seed)
        ks = jax.random.split(key, 8)
        s = 1.0 / np.sqrt(D_IN)
        x = jax.random.normal(ks[0], (N_NODES, D_IN), dtype=jnp.float32)
        edge_index = jax.random.randint(ks[1], (2, N_EDGES), 0, N_NODES, dtype=jnp.int64)
        Wl1 = jax.random.normal(ks[2], (D_OUT, D_IN), dtype=jnp.float32) * s
        Wr1 = jax.random.normal(ks[3], (D_OUT, D_IN), dtype=jnp.float32) * s
        b1 = jnp.zeros((D_OUT,), dtype=jnp.float32)
        Wl2 = jax.random.normal(ks[4], (D_IN, D_OUT), dtype=jnp.float32) * s
        Wr2 = jax.random.normal(ks[5], (D_IN, D_OUT), dtype=jnp.float32) * s
        b2 = jnp.zeros((D_IN,), dtype=jnp.float32)
        return {'x': x, 'edge_index': edge_index, 'Wl1': Wl1, 'Wr1': Wr1, 'b1': b1, 'Wl2': Wl2, 'Wr2': Wr2, 'b2': b2}
    _L1_gnn_all = _L1_gnn_setup()
    _L1_gnn_in = {k: v for k, v in _L1_gnn_all.items() if k in ('Wl1', 'Wr1', 'b1', 'Wl2', 'Wr2', 'b2')}
    del _L1_gnn_all
    return {'x': x, 'src': src, 'dst': dst, 'L0_gnn_t_emb': _L0_gnn_in['t_emb'], 'L0_gnn_W': _L0_gnn_in['W'], 'L0_gnn_b': _L0_gnn_in['b'], 'L0_gnn_Wt': _L0_gnn_in['Wt'], 'L0_gnn_bt': _L0_gnn_in['bt'], 'L1_gnn_Wl1': _L1_gnn_in['Wl1'], 'L1_gnn_Wr1': _L1_gnn_in['Wr1'], 'L1_gnn_b1': _L1_gnn_in['b1'], 'L1_gnn_Wl2': _L1_gnn_in['Wl2'], 'L1_gnn_Wr2': _L1_gnn_in['Wr2'], 'L1_gnn_b2': _L1_gnn_in['b2']}

def reference(x, src, dst, L0_gnn_t_emb, L0_gnn_W, L0_gnn_b, L0_gnn_Wt, L0_gnn_bt, L1_gnn_Wl1, L1_gnn_Wr1, L1_gnn_b1, L1_gnn_Wl2, L1_gnn_Wr2, L1_gnn_b2):
    import jax
    import jax.numpy as jnp

    def _L0_gnn_ref(x, t_emb, edge_index, W, b, Wt, bt):
        import jax, jax.numpy as jnp
        import numpy as np

        def _gcn_conv(x, edge_index, W, b):
            N = x.shape[0]
            loops = jnp.arange(N, dtype=edge_index.dtype)
            src = jnp.concatenate([edge_index[0], loops])
            dst = jnp.concatenate([edge_index[1], loops])
            deg = jax.ops.segment_sum(jnp.ones_like(dst, dtype=x.dtype), dst, num_segments=N)
            dinv = jnp.where(deg > 0, jax.lax.rsqrt(deg), 0.0)
            norm = dinv[src] * dinv[dst]
            xw = x @ W
            msgs = norm[:, None] * xw[src]
            out = jax.ops.segment_sum(msgs, dst, num_segments=N)
            return out + b
        h = _gcn_conv(x, edge_index, W, b)
        time_emb = t_emb @ Wt + bt
        return h + time_emb

    def _L1_gnn_ref(x, edge_index, Wl1, Wr1, b1, Wl2, Wr2, b2):
        import jax, jax.numpy as jnp
        import numpy as np
        N_NODES = 6250
        N_EDGES = 100000
        D_IN = 512
        D_OUT = 512

        def sage_conv(x, src, dst, Wl, Wr, b, num_nodes):
            msg = x[src]
            summed = jax.ops.segment_sum(msg, dst, num_segments=num_nodes)
            cnt = jax.ops.segment_sum(jnp.ones((src.shape[0],), dtype=x.dtype), dst, num_segments=num_nodes)
            mean = summed / jnp.maximum(cnt, 1.0)[:, None]
            return mean @ Wl.T + x @ Wr.T + b
        src, dst = (edge_index[0], edge_index[1])
        n = x.shape[0]
        h = sage_conv(x, src, dst, Wl1, Wr1, b1, n)
        h = jax.nn.relu(h)
        return sage_conv(h, src, dst, Wl2, Wr2, b2, n)
    edge_index = jnp.stack([src, dst])
    x = _layernorm(x + _L0_gnn_ref(x, L0_gnn_t_emb, edge_index, L0_gnn_W, L0_gnn_b, L0_gnn_Wt, L0_gnn_bt), axis=-1)
    x = _layernorm(x + _L1_gnn_ref(x, edge_index, L1_gnn_Wl1, L1_gnn_Wr1, L1_gnn_b1, L1_gnn_Wl2, L1_gnn_Wr2, L1_gnn_b2), axis=-1)
    return x

_drawn_inputs = setup_inputs


def setup_inputs(seed=0):
    import zlib

    import numpy as np

    out = dict(_drawn_inputs(seed))
    spreads = {'L0_gnn_b': (0.0, 0.1),
     'L0_gnn_bt': (0.0, 0.1),
     'L1_gnn_b1': (0.0, 0.1),
     'L1_gnn_b2': (0.0, 0.1)}
    factors = {}
    for name, (base, spread) in spreads.items():
        noise = np.random.default_rng([zlib.crc32(name.encode()), seed]).standard_normal(out[name].shape)
        drawn = base * np.exp(spread * noise) if base else spread * noise
        out[name] = jnp.asarray(drawn.astype(out[name].dtype))
    for name, factor in factors.items():
        out[name] = (out[name] * factor).astype(out[name].dtype)
    return out
```

```python
import concourse.bass as bass
from concourse import mybir
from contextlib import ExitStack


def gnn_resnorm(nc, x, src, dst, t_emb, w0, b0, wt, bt, wl1t, wr1t, b1, wl2t, wr2t, b2, out):
    fp32, f32r, bf16 = mybir.dt.float32, mybir.dt.float32r, mybir.dt.bfloat16
    i32, u16 = mybir.dt.int32, mybir.dt.uint16
    ALU, ACT, AX = mybir.AluOpType, mybir.ActivationFunctionType, mybir.AxisListType

    N, D = x.shape
    E = src.shape[0]
    P = 128
    T = -(-N // P)
    TAIL = N - (T - 1) * P
    KD = D // P
    KE = t_emb.shape[0] // P
    EPS = 1e-5

    CH = 2
    GROUP = CH * P
    NG = -(-E // GROUP)
    SLOTS = 8
    HR = 4
    EVAC, FINISH, ROOT, NORM, STORE = 3, 4, 4, 5, 6
    NS = -(-(NG + T - 1 + STORE + 1) // (2 * SLOTS)) * 2 * SLOTS
    SB = -(-NS // P)
    FPAD = 8
    SKIP = 65535.0
    NL = 3
    EC = -(-E // P)
    HB = 34
    EPAD = (NG + 1) * GROUP
    NB, BT = 7, T // 7
    assert EC % HB == 0 and NB * BT == T and NS % HR == 0 and HB % 2 == 0

    ctx = ExitStack()
    with ctx:
        def sb(name, shape, dt, scope=ctx):
            return scope.enter_context(nc.sbuf_tensor(name, shape, dt))

        def pb(name, shape, dt):
            return ctx.enter_context(nc.psum_tensor(name, shape, dt))

        def sem(name):
            return ctx.enter_context(nc.semaphore(name))

        src_rows = nc.dram_tensor("src_rows", [NG + 1, GROUP], i32, kind="Internal").ap()
        dst_rows = nc.dram_tensor("dst_rows", [NG + 1, GROUP], i32, kind="Internal").ap()
        tables = [nc.dram_tensor(f"table{n}", [(T + 1) * P, D], fp32, kind="Internal").ap() for n in range(NL)]

        X = sb("X", [P, T, D], fp32)
        idx_tab = sb("idx_tab", [P, CH, SB * P], u16)
        loc_tab = sb("loc_tab", [P, CH, SB * P], bf16)
        flags = sb("flags", [1, FPAD + SB * P], i32)
        bias = sb("bias", [P, NL, D], fp32)
        ident = sb("ident", [P, P], fp32)
        iota_row = sb("iota_row", [P, P], fp32)
        zeros = sb("zeros", [P, P], bf16)
        dinv = sb("dinv", [P, T], fp32)
        rcnt = sb("rcnt", [P, T], fp32)
        mv = sb("mv", [P, 2], fp32)
        root = sb("root", [P, 1], fp32)
        rstd = sb("rstd", [P, 1], fp32)
        stats = sb("stats", [P, 6], fp32)
        eps = sb("eps", [P, 1], fp32)
        idx_ring = sb("idx_ring", [P, 2, CH, SLOTS], i32)

        early = ExitStack()
        dst_nat = sb("dst_nat", [P, EC], i32, early)
        dst_hi_i = sb("dst_hi_i", [P, EC], i32, early)
        dst_lo_i = sb("dst_lo_i", [P, EC], i32, early)
        dst_hi = sb("dst_hi", [P, EC], bf16, early)
        dst_lo = sb("dst_lo", [P, EC], bf16, early)
        iota_lo = sb("iota_lo", [P, P, HB], bf16, early)
        oh_lo = sb("oh_lo", [P, 2 * P * HB], bf16, early)
        oh_hi = sb("oh_hi", [P, 2 * T * HB], bf16, early)
        hpad = sb("hpad", [1, EPAD - E], i32, early)
        early.close()

        mid = ExitStack()
        stage = sb("stage", [P, 2, BT, D], fp32, mid)
        srow = sb("srow", [P, SB, GROUP], i32, mid)
        drow = sb("drow", [P, SB, GROUP], i32, mid)
        locf = sb("locf", [P, SB, GROUP], fp32, mid)
        idxf = sb("idxf", [P, SB, GROUP], fp32, mid)
        off_lo = sb("off_lo", [P, SB, GROUP], fp32, mid)
        late_wt = sb("late_wt", [P, KE, D], fp32, mid)
        brow = sb("brow", [P, D], fp32, mid)
        tcol = sb("tcol", [P, KE], fp32, mid)
        tbc = sb("tbc", [P, KE, P], fp32, mid)
        ones = sb("ones", [P, P], fp32, mid)
        cnt = sb("cnt", [P, T], fp32, mid)
        n_t = sb("n_t", [P, T], fp32, mid)
        end_t = sb("end_t", [P, T], fp32, mid)
        grp_f = sb("grp_f", [P, 2, T], fp32, mid)
        grp_i = sb("grp_i", [P, 2, T], i32, mid)
        grp_s = sb("grp_s", [P, 2, T], i32, mid)
        steps_t = sb("steps_t", [P, T], fp32, mid)
        send_t = sb("send_t", [P, T], fp32, mid)
        shift_t = sb("shift_t", [P, T], fp32, mid)
        iota_t = sb("iota_t", [P, T + 1], fp32, mid)
        iota_s = sb("iota_s", [P, SB], fp32, mid)
        pick = sb("pick", [P, 3, SB, T], fp32, mid)
        tile_s = sb("tile_s", [P, SB], fp32, mid)
        base_s = sb("base_s", [P, SB], fp32, mid)
        grp_sf = sb("grp_sf", [P, SB], fp32, mid)
        grp_si = sb("grp_si", [P, SB], i32, mid)
        flag_s = sb("flag_s", [P, SB], fp32, mid)
        next_s = sb("next_s", [P, SB], fp32, mid)
        mid.close()

        hi = sb("hi", [P, HR, CH, D], f32r)
        lo = sb("lo", [P, HR, CH, D], f32r)
        oh = sb("oh", [P, HR, CH, P], f32r)
        W = sb("W", [P, 2, KD, D], fp32)
        selfbuf = sb("selfbuf", [P, D], fp32)
        agg = sb("agg", [P, D], fp32)
        selfT = sb("selfT", [P, D], fp32)
        aggT = sb("aggT", [P, D], fp32)
        hbuf = sb("hbuf", [P, D], fp32)
        raw = sb("raw", [P, SLOTS, CH * D], fp32)

        sum_ps = pb("sum_ps", [P, D], fp32)
        aggT_ps = pb("aggT_ps", [P, D], fp32)
        selfT_ps = pb("selfT_ps", [P, D], fp32)
        prod_ps = pb("prod_ps", [P, D], fp32)
        hist_ps = pb("hist_ps", [P, D], fp32)
        tmp_ps = [pb(f"tmp_ps{n}", [P, D], fp32) for n in range(3)]

        names = """edges_copied pad_made dst_loaded x_loaded consts_made oh_ready oh_used hist_done deg_made
            total_ps sched_ready rows_gathered tabs_ps tabs_read tabs_made loads_done tbc_made bias_ps bias_made
            staged stage_stored0 stage_stored1 zero_stored w_loaded chain raw_done gathered hi_ready onehot_ready
            pe_done self_loaded self_read selfT_ready agg_ready aggT_done aggT_ready prod_ready prod_read sum_chain
            stats_ready root_ready rstd_ready norm_ready x_stored h_stored h_ready idx_copied
            out_stored flags_ps stats_made slot_claimed x_tail_zero""".split()
        S = {n: sem(n) for n in names}
        slot_full = [sem(f"slot_full{n}") for n in range(SLOTS)]

        block = ctx.enter_context(nc.Block())

        X2 = X[:, :, :].rearrange("p t d -> p (t d)")
        raw2 = raw[:, :, :].rearrange("p n d -> p (n d)")

        def tile_of_x(t1):
            return X2[:, bass.ds(t1 * D - D, D)]

        def raw_slot(b, r):
            return raw2[:, bass.ds((b % (SLOTS // HR)) * (HR * CH * D) + r * CH * D, CH * D)].rearrange("p (j d) -> p j d", j=CH)

        def flagged(t1, most=T):
            return nc.s_assert_within(t1, 1, most, skip_runtime_bounds_check_because="the flag is not zero here")

        def flag_regs(eng, s, lag):
            return [eng.value_load(flags[0:1, bass.ds(s + (FPAD - lag + r), 1)], min_val=0, max_val=T)
                    for r in range(HR)]

        @block.sync
        def _(sp):
            full = E // GROUP * GROUP
            for rows, edges in ((src_rows, src), (dst_rows, dst)):
                flat = rows.rearrange("g e -> (g e)")
                sp.dma_start(flat[0:full].rearrange("(g e) -> g e", e=GROUP),
                             edges[0:full].rearrange("(g e) -> g e", e=GROUP)).then_inc(S["edges_copied"], 16)
                sp.dma_start(flat[full:E].rearrange("(a e) -> a e", a=1),
                             edges[full:E].rearrange("(a e) -> a e", a=1)).then_inc(S["edges_copied"], 16)
                if rows is src_rows:
                    sp.wait_ge(S["pad_made"], 1)
                sp.dma_start(flat[E:EPAD].rearrange("(a e) -> a e", a=1),
                             hpad[0:1, 0:EPAD - E]).then_inc(S["edges_copied"], 16)
            sp.wait_ge(S["edges_copied"], 6 * 16)
            flat = dst_rows.rearrange("g e -> (g e)")
            sp.dma_start(dst_nat[:, :], flat[0:P * EC].rearrange("(p c) -> p c", p=P)).then_inc(S["dst_loaded"], 16)
            sp.wait_ge(S["x_tail_zero"], 1)
            sp.dma_start(X[0:TAIL, T - 1, :], x[(T - 1) * P:N, :]).then_inc(S["x_loaded"], 16)
            for a in range(0, T - 1, 8):
                sp.dma_start(X[:, a:a + 8, :],
                             x[a * P:(a + 8) * P, :].rearrange("(t p) d -> p t d", p=P)).then_inc(S["x_loaded"], 16)
            sp.wait_ge(S["hist_done"], 1)
            for p0, row in ((0, b0), (1, bt), (32, b1), (64, b2)):
                sp.dma_start(brow[p0:p0 + 1, :], row.rearrange("(a d) -> a d", a=1)).then_inc(S["loads_done"], 16)
            for k in range(KE):
                sp.dma_start(tcol[:, k:k + 1],
                             t_emb[k * P:(k + 1) * P].rearrange("(p a) -> p a", a=1)).then_inc(S["loads_done"], 16)
            sp.dma_start(late_wt[:, :, :], wt.rearrange("(k p) d -> p k d", p=P)).then_inc(S["loads_done"], 16)
            for L in range(NL):
                if L == 0:
                    sp.wait_ge(S["tabs_made"], 1)
                    sp.wait_ge(S["bias_made"], 1)
                    sp.wait_ge(S["stage_stored0"], 16 * 4)
                    sp.wait_ge(S["stage_stored1"], 16 * 3)
                    sp.dma_start(W[:, 0, :, :], w0.rearrange("(k p) d -> p k d", p=P)).then_inc(S["w_loaded"], 16)
                else:
                    sp.wait_ge(S["prod_ready"], T * L)
                    for n, w in enumerate(((wl1t, wr1t), (wl2t, wr2t))[L - 1]):
                        sp.dma_start(W[:, n, :, :],
                                     w.rearrange("(k p) d -> p k d", p=P)).then_inc(S["w_loaded"], 16)
                with sp.Fori(0, NS, SLOTS) as s:
                    for n in range(SLOTS):
                        sp.wait_ge(slot_full[n], s * (16 * CH // SLOTS) + 16 * CH * (NS // SLOTS * L + 1))
                        sp.sem_inc(S["gathered"], 1)

        @block.gpsimd
        def _(pool):
            nc.gpsimd.memset(hpad[0:1, :], -1).then_inc(S["pad_made"], 1)
            nc.gpsimd.memset(X[:, T - 1, :], 0.0).then_inc(S["x_tail_zero"], 1)
            nc.gpsimd.iota(iota_lo[:, :, :], [[1, P], [0, HB]], base=0, channel_multiplier=0,
                           allow_small_or_imprecise_dtypes=True)
            nc.gpsimd.memset(zeros[:, :], 0.0)
            nc.gpsimd.memset(flags[0:1, 0:FPAD], 0)
            nc.gpsimd.memset(eps[:, :], EPS)
            nc.gpsimd.memset(ident[:, :], 0.0)
            nc.gpsimd.iota(iota_row[:, :], [[1, P]], base=0, channel_multiplier=0,
                           allow_small_or_imprecise_dtypes=True).then_inc(S["consts_made"], 1)
            pool.wait_ge(S["consts_made"], 1)
            nc.gpsimd.affine_select(out=ident[:, :], in_=ident[:, :], compare_op=ALU.not_equal, fill=1.0, base=0,
                                    pattern=[[-1, P]], channel_multiplier=1).then_inc(S["consts_made"], 1)
            pool.wait_ge(S["hist_done"], 1)
            nc.gpsimd.memset(ones[:, :], 1.0)
            nc.gpsimd.iota(iota_t[:, :], [[1, T + 1]], base=0, channel_multiplier=0,
                           allow_small_or_imprecise_dtypes=True)
            nc.gpsimd.iota(iota_s[:, :], [[P, SB]], base=0, channel_multiplier=1,
                           allow_small_or_imprecise_dtypes=True).then_inc(S["consts_made"], 1)
            nc.gpsimd.memset(raw[:, :, :], 0.0).then_inc(S["raw_done"], SLOTS)
            pool.wait_ge(S["sched_ready"], 1)
            for q in range(SB):
                for rows, buf in ((src_rows, srow), (dst_rows, drow)):
                    nc.gpsimd.indirect_dma_start(
                        out=buf[:, q, :], out_offset=None, in_=rows[:, :],
                        in_offset=bass.IndirectOffsetOnAxis(ap=grp_si[:, q:q + 1], axis=0),
                    ).then_inc(S["rows_gathered"], 16)
            pool.wait_ge(S["tabs_made"], 1)
            pool.wait_ge(S["zero_stored"], 16 * NL)
            last_row = pool.to_reg(N - 1)
            for L in range(NL):
                if L == 0:
                    pool.wait_ge(S["stage_stored0"], 16 * 4)
                    pool.wait_ge(S["stage_stored1"], 16 * 3)
                elif L == 1:
                    pool.wait_ge(S["x_stored"], 16 * T)
                else:
                    pool.wait_ge(S["h_stored"], 16 * (T + 1))
                with pool.Fori(0, NS, 2 * SLOTS) as s:
                    for half in range(2):
                        nc.gpsimd.tensor_copy(idx_ring[:, half, :, :],
                                              idx_tab[:, :, bass.ds(s + half * SLOTS, SLOTS)]).then_inc(
                                                  S["idx_copied"], SLOTS)
                        pool.wait_ge(S["idx_copied"], s + (NS * L + (half + 1) * SLOTS))
                        for n in range(SLOTS):
                            pool.wait_ge(S["raw_done"], s + (NS * L + half * SLOTS + n + 1))
                            pool.sem_inc(S["slot_claimed"], 1)
                            for j in range(CH):
                                nc.gpsimd.indirect_dma_start(
                                    out=raw[:, n, j * D:(j + 1) * D], out_offset=None, in_=tables[L][:, :],
                                    in_offset=bass.IndirectOffsetOnAxis(ap=idx_ring[:, half, j, n:n + 1], axis=0),
                                    bounds_check=last_row, oob_is_err=False,
                                ).then_inc(slot_full[n], 16)

        @block.vector
        def _(dve):
            v = nc.vector
            count = [0]

            def link(ins):
                count[0] += 1
                ins.then_inc(S["chain"], 1)
                dve.wait_ge(S["chain"], count[0])

            dve.sem_inc(S["prod_read"], 1)
            dve.sem_inc(S["sum_chain"], 1)
            dve.wait_ge(S["dst_loaded"], 16)
            v.tensor_scalar(dst_hi_i[:, :], dst_nat[:, :], 7, None, ALU.arith_shift_right)
            link(v.tensor_scalar(dst_lo_i[:, :], dst_nat[:, :], P - 1, None, ALU.bitwise_and))
            v.tensor_copy(dst_hi[:, :], dst_hi_i[:, :])
            link(v.tensor_copy(dst_lo[:, :], dst_lo_i[:, :]))
            dve.wait_ge(S["consts_made"], 1)
            with dve.Fori(0, EC // HB) as b:
                dve.wait_ge(S["oh_used"], b + 1)
                lo_b = dst_lo[:, bass.ds(b * HB, HB)].unsqueeze(1).to_broadcast([P, P, HB])
                hi_b = dst_hi[:, bass.ds(b * HB, HB)].unsqueeze(1).to_broadcast([P, T, HB])
                v.tensor_tensor(oh_lo[:, bass.ds((b % 2) * (P * HB), P * HB)].rearrange("p (a c) -> p a c", c=HB),
                                iota_lo[:, :, :], lo_b, ALU.is_equal)
                v.tensor_tensor(oh_hi[:, bass.ds((b % 2) * (T * HB), T * HB)].rearrange("p (a c) -> p a c", c=HB),
                                iota_lo[:, 0:T, :], hi_b, ALU.is_equal).then_inc(S["oh_ready"], 1)
            dve.wait_ge(S["hist_done"], 1)
            dve.wait_ge(S["consts_made"], 3)
            link(v.tensor_copy(cnt[:, :], hist_ps[:, 0:T]))
            link(v.tensor_scalar(rcnt[:, :], cnt[:, :], 1.0, None, ALU.max))
            v.tensor_scalar(dinv[:, :], cnt[:, :], 1.0, None, ALU.add).then_inc(S["deg_made"], 1)
            link(v.reciprocal(rcnt[:, :], rcnt[:, :]))
            dve.wait_ge(S["deg_made"], 2)
            v.reciprocal(dinv[:, :], dinv[:, :]).then_inc(S["deg_made"], 1)
            dve.wait_ge(S["total_ps"], 1)
            link(v.tensor_copy(n_t[:, :], tmp_ps[0][:, 0:T]))
            link(v.tensor_tensor_scan(end_t[:, :], ones[:, 0:T], n_t[:, :], 0.0, ALU.mult, ALU.add))
            v.tensor_tensor(grp_f[:, 0, :], end_t[:, :], n_t[:, :], ALU.subtract)
            link(v.tensor_scalar(grp_f[:, 1, :], end_t[:, :], -1.0, None, ALU.add))
            link(v.tensor_copy(grp_i[:, :, :], grp_f[:, :, :]))
            link(v.tensor_scalar(grp_s[:, :, :], grp_i[:, :, :], 8, None, ALU.arith_shift_right))
            link(v.tensor_copy(grp_f[:, :, :], grp_s[:, :, :]))
            link(v.tensor_tensor(steps_t[:, :], grp_f[:, 1, :], grp_f[:, 0, :], ALU.subtract))
            link(v.tensor_scalar(steps_t[:, :], steps_t[:, :], 1.0, 1.0, ALU.add, ALU.max))
            link(v.tensor_tensor_scan(send_t[:, :], ones[:, 0:T], steps_t[:, :], 0.0, ALU.mult, ALU.add))
            link(v.tensor_tensor(shift_t[:, :], grp_f[:, 0, :], send_t[:, :], ALU.subtract))
            v.tensor_tensor(shift_t[:, :], shift_t[:, :], steps_t[:, :], ALU.add)
            link(v.tensor_scalar(next_s[:, :], iota_s[:, :], 1.0, None, ALU.add))
            for q in range(SB):
                v.tensor_scalar(pick[:, 0, q, 0:T - 1], send_t[:, 0:T - 1], iota_s[:, q:q + 1], 0.0, ALU.is_le,
                                ALU.add, accum_out=tile_s[:, q:q + 1])
                last = v.scalar_tensor_tensor(pick[:, 1, q, :], send_t[:, :], next_s[:, q:q + 1], iota_t[:, 1:T + 1],
                                              ALU.is_equal, ALU.mult, accum_out=flag_s[:, q:q + 1])
            link(last)
            for q in range(SB):
                last = v.scalar_tensor_tensor(pick[:, 2, q, :], iota_t[:, 0:T], tile_s[:, q:q + 1], shift_t[:, :],
                                              ALU.is_equal, ALU.mult, accum_out=base_s[:, q:q + 1])
            link(last)
            link(v.tensor_tensor(grp_sf[:, :], base_s[:, :], iota_s[:, :], ALU.add))
            link(v.tensor_scalar(grp_sf[:, :], grp_sf[:, :], float(NG), 0.0, ALU.min, ALU.max))
            v.tensor_scalar(tile_s[:, :], tile_s[:, :], float(P), None, ALU.mult)
            v.tensor_copy(grp_si[:, :], grp_sf[:, :]).then_inc(S["sched_ready"], 1)
            dve.wait_ge(S["loads_done"], 16 * (5 + KE))
            v.tensor_copy(tbc[:, :, :], tcol[:, :].unsqueeze(2).to_broadcast([P, KE, P])).then_inc(S["tbc_made"], 1)
            dve.wait_ge(S["bias_ps"], 1)
            for n in range(NL):
                last = v.tensor_copy(bias[:, n, :], tmp_ps[n][:, :])
            last.then_inc(S["bias_made"], 1)
            dve.wait_ge(S["rows_gathered"], 16 * 2 * SB)
            for q in range(SB):
                last = v.tensor_scalar(locf[:, q, :], drow[:, q, :], tile_s[:, q:q + 1], None, ALU.subtract)
            link(last)
            v.tensor_scalar(off_lo[:, :, :], locf[:, :, :], 0.0, SKIP, ALU.is_lt, ALU.mult)
            link(v.tensor_scalar(idxf[:, :, :], locf[:, :, :], float(P - 1), SKIP, ALU.is_gt, ALU.mult))
            link(v.tensor_tensor(idxf[:, :, :], idxf[:, :, :], off_lo[:, :, :], ALU.add))
            link(v.tensor_tensor(idxf[:, :, :], idxf[:, :, :], srow[:, :, :], ALU.add))
            v.tensor_scalar(idxf[:, :, :], idxf[:, :, :], SKIP, None, ALU.min)
            v.tensor_scalar(locf[:, :, :], locf[:, :, :], -1.0, float(P), ALU.max, ALU.min).then_inc(S["tabs_ps"], 1)
            for j in range(CH):
                dve.wait_ge(S["tabs_ps"], 2 + j)
                v.tensor_copy(idx_tab[:, j, :], tmp_ps[0][:, :])
                v.tensor_copy(loc_tab[:, j, :], tmp_ps[1][:, :]).then_inc(S["tabs_read"], 1)
            dve.wait_ge(S["flags_ps"], 1)
            v.tensor_copy(flags[0:1, FPAD:FPAD + SB * P], tmp_ps[2][0:1, :]).then_inc(S["tabs_made"], 1)
            dve.wait_ge(S["tabs_made"], 1)
            dve.wait_ge(S["stage_stored0"], 16 * 4)
            dve.wait_ge(S["stage_stored1"], 16 * 3)

            def norm(L, t1):
                ends = L // 2 * T
                dve.wait_ge(S["root_ready"], t1 + ends)
                v.reciprocal(rstd[:, :], root[:, :]).then_inc(S["rstd_ready"], 1)
                dve.wait_ge(S["rstd_ready"], t1 + ends)
                v.tensor_scalar(tile_of_x(t1), hbuf[:, :], mv[:, 0:1], rstd[:, :], ALU.subtract,
                                ALU.mult).then_inc(S["norm_ready"], 1)

            def finish(L, t1):
                dve.wait_ge(S["prod_ready"], t1 + T * L)
                if L == 1:
                    dve.wait_ge(S["h_stored"], t1 * 16)
                    v.tensor_tensor(hbuf[:, :], prod_ps[:, :], bias[:, 1, :], ALU.add).then_inc(S["prod_read"], 1)
                    return
                ends = L // 2 * T
                v.tensor_tensor(hbuf[:, :], prod_ps[:, :], tile_of_x(t1), ALU.add).then_inc(S["prod_read"], 1)
                dve.wait_ge(S["prod_read"], t1 + (T * L + 1))
                v.tensor_tensor(hbuf[:, :], hbuf[:, :], bias[:, L, :], ALU.add).then_inc(S["sum_chain"], 1)
                dve.wait_ge(S["sum_chain"], t1 * 2 + 2 * ends)
                v.bn_stats(stats[:, :], hbuf[:, :]).then_inc(S["sum_chain"], 1)
                dve.wait_ge(S["sum_chain"], t1 * 2 + (2 * ends + 1))
                dve.sem_inc(S["stats_made"], 1)
                v.bn_aggr(mv[:, :], stats[:, :]).then_inc(S["stats_ready"], 1)

            for L in range(NL):
                with dve.Fori(0, NS // HR) as b:
                    s = b * HR
                    done = flag_regs(dve, s, FINISH)
                    normed = flag_regs(dve, s, NORM) if L != 1 else None
                    for r in range(HR):
                        step = s + (NS * L + r + 1)
                        dve.wait_ge(S["pe_done"], step)
                        for j in range(CH):
                            last = v.tensor_scalar(oh[:, r, j, :], iota_row[:, :],
                                                   loc_tab[:, j, bass.ds(s + r, 1)], None, ALU.is_equal)
                        last.then_inc(S["onehot_ready"], 1)
                        dve.wait_ge(S["hi_ready"], step)
                        v.tensor_tensor(lo[:, r, :, :], raw_slot(b, r), hi[:, r, :, :].bitcast(fp32),
                                        ALU.subtract).then_inc(S["raw_done"], 1)
                        if L != 1:
                            with dve.If(normed[r] > 0):
                                norm(L, flagged(normed[r]))
                        with dve.If(done[r] > 0):
                            finish(L, flagged(done[r]))

        @block.scalar
        def _(act):
            a = nc.scalar
            act.sem_inc(S["h_stored"], 16)
            act.wait_ge(S["consts_made"], 1)
            act.wait_ge(S["deg_made"], 1)
            a.activation(dinv[:, :], dinv[:, :], ACT.Sqrt).then_inc(S["deg_made"], 1)
            act.wait_ge(S["deg_made"], 3)
            act.wait_ge(S["x_loaded"], 16 * (1 + (T - 1) // 8))
            stored = (S["stage_stored0"], S["stage_stored1"])
            for b in range(NB):
                if b >= 2:
                    act.wait_ge(stored[b % 2], 16 * (b // 2))
                for k in range(BT):
                    t = b * BT + k
                    last = a.activation(stage[:, b % 2, k, :], X[:, t, :], ACT.Copy, scale=dinv[:, t:t + 1])
                last.then_inc(S["staged"], 1)
                act.wait_ge(S["staged"], b + 1)
                act.dma_start(tables[0][b * BT * P:(b + 1) * BT * P, :].rearrange("(t p) d -> p t d", p=P),
                              stage[:, b % 2, :, :]).then_inc(stored[b % 2], 16)
            act.wait_ge(S["raw_done"], SLOTS)
            for n in range(NL):
                act.dma_start(tables[n][T * P:(T + 1) * P, :], raw[:, 0, 0:D]).then_inc(S["zero_stored"], 16)
            act.wait_ge(S["zero_stored"], 16 * NL)
            act.wait_ge(S["tabs_made"], 1)
            act.wait_ge(S["bias_made"], 1)
            act.wait_ge(S["stage_stored0"], 16 * 4)
            act.wait_ge(S["stage_stored1"], 16 * 3)

            def flush(L, t1):
                scale = (dinv, rcnt, rcnt)[L]
                act.wait_ge(S["self_read"], t1 + T * L)
                a.activation(agg[:, :], sum_ps[:, :], ACT.Copy,
                             scale=scale[:, bass.ds(t1 - 1, 1)]).then_inc(S["agg_ready"], 1)
                act.dma_start(selfbuf[:, :], tables[L][bass.ds(t1 * P, P), :]).then_inc(S["self_loaded"], 16)
                if L > 0:
                    a.activation(selfT[:, :], selfT_ps[:, :], ACT.Copy).then_inc(S["selfT_ready"], 1)
                act.wait_ge(S["aggT_done"], t1 + T * L)
                a.activation(aggT[:, :], aggT_ps[:, :], ACT.Copy).then_inc(S["aggT_ready"], 1)

            def square_root(L, t1):
                ends = L // 2 * T
                if L == 1:
                    act.wait_ge(S["prod_read"], t1 + (T * L + 1))
                    a.activation(hbuf[:, :], hbuf[:, :], ACT.Relu).then_inc(S["h_ready"], 1)
                    act.wait_ge(S["h_ready"], t1)
                    act.dma_start(tables[2][bass.ds(t1 * P - P, P), :], hbuf[:, :]).then_inc(S["h_stored"], 16)
                    return
                act.wait_ge(S["stats_ready"], t1 + ends)
                a.activation(root[:, :], mv[:, 1:2], ACT.Sqrt,
                             bias=eps[:, 0:1]).then_inc(S["root_ready"], 1)

            def store(L, t1):
                act.wait_ge(S["norm_ready"], t1 + L // 2 * T)
                if L == 0:
                    act.dma_start(tables[1][bass.ds(t1 * P - P, P), :], tile_of_x(t1)).then_inc(S["x_stored"], 16)
                else:
                    act.dma_start(out[bass.ds(t1 * P - P, P), :], tile_of_x(t1)).then_inc(S["out_stored"], 16)

            for L in range(NL):
                if L == 1:
                    act.wait_ge(S["x_stored"], 16 * T)
                elif L == 2:
                    act.wait_ge(S["h_stored"], 16 * (T + 1))
                if L > 0:
                    act.wait_ge(S["self_loaded"], 16 * (T + 1) * L)
                act.dma_start(selfbuf[:, :], tables[L][0:P, :]).then_inc(S["self_loaded"], 16)
                with act.Fori(0, NS // HR) as b:
                    s = b * HR
                    flushed = flag_regs(act, s, EVAC)
                    rooted = flag_regs(act, s, ROOT)
                    stores = flag_regs(act, s, STORE) if L != 1 else None
                    for r in range(HR):
                        step = s + (NS * L + r + 1)
                        act.wait_ge(S["gathered"], step)
                        act.wait_ge(S["pe_done"], step)
                        a.activation(hi[:, r, :, :], raw_slot(b, r), ACT.Copy).then_inc(S["hi_ready"], 1)
                        with act.If(flushed[r] > 0):
                            flush(L, flagged(flushed[r]))
                        with act.If(rooted[r] > 0):
                            square_root(L, flagged(rooted[r]))
                        if L == 0:
                            with act.If(stores[r] > 0):
                                store(L, flagged(stores[r]))
                        if L == 2:
                            with act.If(stores[r] * (T - stores[r]) > 0):
                                store(L, flagged(stores[r], T - 1))
            act.wait_ge(S["norm_ready"], 2 * T)
            act.dma_start(out[(T - 1) * P:N, :], X[0:TAIL, T - 1, :]).then_inc(S["out_stored"], 16)
            act.wait_ge(S["out_stored"], 16 * T)
            act.wait_ge(S["self_loaded"], 16 * (T + 1) * NL)

        @block.tensor
        def _(pe):
            mm = nc.tensor.matmul

            def clear(bank, cols, n=1):
                return mm(bank[:, 0:cols], zeros[:, :], zeros[:, 0:1].to_broadcast([P, cols]), start=True, stop=False,
                          skip_group_check=True)

            pe.sem_inc(S["oh_used"], 2)
            pe.sem_inc(S["pe_done"], HR)
            pe.wait_ge(S["consts_made"], 2)
            clear(hist_ps, T)
            with pe.Fori(0, EC // HB) as b:
                pe.wait_ge(S["oh_ready"], b + 1)
                lo_b = oh_lo[:, bass.ds((b % 2) * (P * HB), P * HB)].rearrange("p (a c) -> p a c", c=HB)
                hi_b = oh_hi[:, bass.ds((b % 2) * (T * HB), T * HB)].rearrange("p (a c) -> p a c", c=HB)
                for c in range(HB):
                    last = mm(hist_ps[:, 0:T], lo_b[:, :, c], hi_b[:, :, c], start=False, stop=False,
                              skip_group_check=True)
                last.then_inc(S["oh_used"], 1)
            mm(hist_ps[:, 0:T], zeros[:, :], zeros[:, 0:T], start=False, stop=True,
               skip_group_check=True).then_inc(S["hist_done"], 1)
            pe.wait_ge(S["consts_made"], 3)
            pe.wait_ge(S["deg_made"], 1)
            mm(tmp_ps[0][:, 0:T], ones[:, :], cnt[:, :], start=True, stop=True).then_inc(S["total_ps"], 1)
            pe.wait_ge(S["tbc_made"], 1)
            for k in range(KE):
                mm(tmp_ps[0][:, :], tbc[:, k, :], late_wt[:, k, :], start=(k == 0), stop=False)
            mm(tmp_ps[0][:, :], ones[0:2, :], brow[0:2, :], start=False, stop=True)
            mm(tmp_ps[1][:, :], ones[32:33, :], brow[32:33, :], start=True, stop=True)
            mm(tmp_ps[2][:, :], ones[64:65, :], brow[64:65, :], start=True, stop=True).then_inc(S["bias_ps"], 1)
            pe.wait_ge(S["bias_made"], 1)
            pe.wait_ge(S["tabs_ps"], 1)
            for q in range(SB):
                last = nc.tensor.transpose(tmp_ps[2][0:1, q * P:(q + 1) * P], flag_s[:, q:q + 1], ident[:, :])
            last.then_inc(S["flags_ps"], 1)
            for j in range(CH):
                if j > 0:
                    pe.wait_ge(S["tabs_read"], j)
                for q in range(SB):
                    nc.tensor.transpose(tmp_ps[0][:, q * P:(q + 1) * P], idxf[:, q, j * P:(j + 1) * P], ident[:, :])
                for q in range(SB):
                    last = nc.tensor.transpose(tmp_ps[1][:, q * P:(q + 1) * P], locf[:, q, j * P:(j + 1) * P],
                                               ident[:, :])
                last.then_inc(S["tabs_ps"], 1)
            pe.wait_ge(S["tabs_made"], 1)

            def flush(L, t1):
                tile = t1 + T * L
                pe.wait_ge(S["self_loaded"], (t1 + (T + 1) * L) * 16)
                if L == 0:
                    mm(sum_ps[:, :], ident[:, :], selfbuf[:, :], start=False, stop=True,
                       skip_group_check=True).then_inc(S["self_read"], 1)
                else:
                    for k in range(KD):
                        last = nc.tensor.transpose(selfT_ps[:, k * P:(k + 1) * P], selfbuf[:, k * P:(k + 1) * P],
                                                   ident[:, :])
                    last.then_inc(S["self_read"], 1)
                pe.wait_ge(S["agg_ready"], tile)
                for k in range(KD):
                    last = nc.tensor.transpose(aggT_ps[:, k * P:(k + 1) * P], agg[:, k * P:(k + 1) * P], ident[:, :])
                last.then_inc(S["aggT_done"], 1)
                clear(sum_ps, D)
                pe.wait_ge(S["prod_read"], tile)
                if L > 0:
                    pe.wait_ge(S["selfT_ready"], tile - T)
                    for k in range(KD):
                        mm(prod_ps[:, :], selfT[:, k * P:(k + 1) * P], W[:, 1, k, :], start=(k == 0), stop=False)
                pe.wait_ge(S["aggT_ready"], tile)
                for k in range(KD):
                    last = mm(prod_ps[:, :], aggT[:, k * P:(k + 1) * P], W[:, 0, k, :], start=(L == 0 and k == 0),
                              stop=(k == KD - 1))
                last.then_inc(S["prod_ready"], 1)

            clear(sum_ps, D)
            for L in range(NL):
                pe.wait_ge(S["w_loaded"], 16 * (1 + 2 * L))
                with pe.Fori(0, NS // HR) as b:
                    s = b * HR
                    ended = flag_regs(pe, s, 0)
                    for r in range(HR):
                        step = s + (NS * L + r + 1)
                        pe.wait_ge(S["onehot_ready"], step)
                        pe.wait_ge(S["hi_ready"], step)
                        for j in range(CH):
                            mm(sum_ps[:, :], oh[:, r, j, :], hi[:, r, j, :], start=False, stop=False,
                               skip_group_check=True)
                        pe.wait_ge(S["raw_done"], step + SLOTS)
                        for j in range(CH):
                            last = mm(sum_ps[:, :], oh[:, r, j, :], lo[:, r, j, :], start=False, stop=False,
                                      skip_group_check=True)
                        last.then_inc(S["pe_done"], 1)
                        with pe.If(ended[r] > 0):
                            flush(L, flagged(ended[r]))


_INS = ['x', 'src', 'dst', 'L0_gnn_t_emb', 'L0_gnn_W', 'L0_gnn_b', 'L0_gnn_Wt', 'L0_gnn_bt', 'L1_gnn_Wl1', 'L1_gnn_Wr1',
        'L1_gnn_b1', 'L1_gnn_Wl2', 'L1_gnn_Wr2', 'L1_gnn_b2']
_TRANSPOSED = ('L1_gnn_Wl1', 'L1_gnn_Wr1', 'L1_gnn_Wl2', 'L1_gnn_Wr2')


def build(nc, arrays):
    args = [nc.dram_tensor(f"in_{n}", arrays[f"in_{n}"].shape, mybir.dt.from_np(arrays[f"in_{n}"].dtype),
                           kind="ExternalInput").ap() for n in _INS]
    out = nc.dram_tensor("out_0", arrays["in_x"].shape, mybir.dt.float32, kind="ExternalOutput").ap()
    gnn_resnorm(nc, *args, out)


def kernel(**inputs):
    import numpy as np
    import concourse.bacc as bacc
    from concourse.bass_utils import run_bass_kernel_spmd

    nc = bacc.Bacc("TRN2", target_bir_lowering=False, num_devices=1)
    arrays = {}
    for n in _INS:
        w = np.asarray(inputs[n])
        arrays[f"in_{n}"] = np.ascontiguousarray(w.T if n in _TRANSPOSED else w)
    build(nc, arrays)
    return run_bass_kernel_spmd(nc, [arrays], core_ids=[0]).results[0]["out_0"]
```

```python
import concourse.bass as bass
from concourse import mybir
from contextlib import ExitStack


def gnn_resnorm(nc, x, src, dst, t_emb, w0, b0, wt, bt, wl1t, wr1t, b1, wl2t, wr2t, b2, out):
    fp32, f32r, bf16 = mybir.dt.float32, mybir.dt.float32r, mybir.dt.bfloat16
    i32, u16 = mybir.dt.int32, mybir.dt.uint16
    ALU, ACT, AX = mybir.AluOpType, mybir.ActivationFunctionType, mybir.AxisListType

    N, D = x.shape
    E = src.shape[0]
    P = 128
    T = -(-N // P)
    TAIL = N - (T - 1) * P
    KD = D // P
    KE = t_emb.shape[0] // P
    EPS = 1e-5

    CH = 2
    GROUP = CH * P
    NG = -(-E // GROUP)
    SLOTS = 8
    HR = 4
    NS = -(-(NG + T - 1) // SLOTS) * SLOTS
    NW = NS // HR
    SB = -(-NS // P)
    PR = 4
    WPAD = 3
    SKIP = 65535.0
    NL = 3
    EC = -(-E // P)
    HB = 34
    EPAD = (NG + 1) * GROUP
    NB, BT = 7, T // 7
    assert EC % HB == 0 and NB * BT == T and NS % HR == 0 and HB % 2 == 0

    ctx = ExitStack()
    with ctx:
        def sb(name, shape, dt, scope=ctx):
            return scope.enter_context(nc.sbuf_tensor(name, shape, dt))

        def pb(name, shape, dt):
            return ctx.enter_context(nc.psum_tensor(name, shape, dt))

        def sem(name):
            return ctx.enter_context(nc.semaphore(name))

        src_rows = nc.dram_tensor("src_rows", [NG + 1, GROUP], i32, kind="Internal").ap()
        dst_rows = nc.dram_tensor("dst_rows", [NG + 1, GROUP], i32, kind="Internal").ap()
        tables = [nc.dram_tensor(f"table{n}", [(T + 1) * P, D], fp32, kind="Internal").ap() for n in range(NL)]

        X = sb("X", [P, T, D], fp32)
        idx_tab = sb("idx_tab", [P, CH, SB * P], u16)
        loc_tab = sb("loc_tab", [P, CH, SB * P], bf16)
        flags = sb("flags", [1, SB * P], i32)
        ended = sb("ended", [1, WPAD + P], i32)
        bias = sb("bias", [P, NL, D], fp32)
        ident = sb("ident", [P, P], fp32)
        iota_row = sb("iota_row", [P, P], fp32)
        zeros = sb("zeros", [P, P], bf16)
        dinv = sb("dinv", [P, T], fp32)
        rcnt = sb("rcnt", [P, T], fp32)
        mv = sb("mv", [P, 2], fp32)
        root = sb("root", [P, 1], fp32)
        rstd = sb("rstd", [P, 1], fp32)
        stats = sb("stats", [P, 6], fp32)
        eps = sb("eps", [P, 1], fp32)
        idx_ring = sb("idx_ring", [P, 2, CH, SLOTS], i32)

        early = ExitStack()
        dst_nat = sb("dst_nat", [P, EC], i32, early)
        dst_hi_i = sb("dst_hi_i", [P, EC], i32, early)
        dst_lo_i = sb("dst_lo_i", [P, EC], i32, early)
        dst_hi = sb("dst_hi", [P, EC], bf16, early)
        dst_lo = sb("dst_lo", [P, EC], bf16, early)
        iota_lo = sb("iota_lo", [P, P, HB], bf16, early)
        oh_lo = sb("oh_lo", [P, 2 * P * HB], bf16, early)
        oh_hi = sb("oh_hi", [P, 2 * T * HB], bf16, early)
        hpad = sb("hpad", [1, EPAD - E], i32, early)
        early.close()

        mid = ExitStack()
        stage = sb("stage", [P, 2, BT, D], fp32, mid)
        srow = sb("srow", [P, SB, GROUP], i32, mid)
        drow = sb("drow", [P, SB, GROUP], i32, mid)
        locf = sb("locf", [P, SB, GROUP], fp32, mid)
        idxf = sb("idxf", [P, SB, GROUP], fp32, mid)
        off_lo = sb("off_lo", [P, SB, GROUP], fp32, mid)
        late_wt = sb("late_wt", [P, KE, D], fp32, mid)
        brow = sb("brow", [P, D], fp32, mid)
        tcol = sb("tcol", [P, KE], fp32, mid)
        tbc = sb("tbc", [P, KE, P], fp32, mid)
        ones = sb("ones", [P, P], fp32, mid)
        cnt = sb("cnt", [P, T], fp32, mid)
        n_t = sb("n_t", [P, T], fp32, mid)
        end_t = sb("end_t", [P, T], fp32, mid)
        grp_f = sb("grp_f", [P, 2, T], fp32, mid)
        grp_i = sb("grp_i", [P, 2, T], i32, mid)
        grp_s = sb("grp_s", [P, 2, T], i32, mid)
        steps_t = sb("steps_t", [P, T], fp32, mid)
        send_t = sb("send_t", [P, T], fp32, mid)
        shift_t = sb("shift_t", [P, T], fp32, mid)
        iota_t = sb("iota_t", [P, T + 1], fp32, mid)
        iota_s = sb("iota_s", [P, SB], fp32, mid)
        pick = sb("pick", [P, 3, SB, T], fp32, mid)
        tile_s = sb("tile_s", [P, SB], fp32, mid)
        base_s = sb("base_s", [P, SB], fp32, mid)
        grp_sf = sb("grp_sf", [P, SB], fp32, mid)
        grp_si = sb("grp_si", [P, SB], i32, mid)
        flag_s = sb("flag_s", [P, SB], fp32, mid)
        next_s = sb("next_s", [P, SB], fp32, mid)
        ended_w = sb("ended_w", [P, 1], fp32, mid)
        win_end = sb("win_end", [P, 1], fp32, mid)
        mid.close()

        hi = sb("hi", [P, HR, CH, D], f32r)
        lo = sb("lo", [P, HR, CH, D], f32r)
        oh = sb("oh", [P, HR, CH, P], f32r)
        W = sb("W", [P, 2, KD, D], fp32)
        selfbuf = sb("selfbuf", [P, D], fp32)
        agg = sb("agg", [P, D], fp32)
        selfT = sb("selfT", [P, D], fp32)
        aggT = sb("aggT", [P, D], fp32)
        hbuf = sb("hbuf", [P, D], fp32)
        raw = sb("raw", [P, SLOTS, CH * D], fp32)

        sum_ps = pb("sum_ps", [P, D], fp32)
        aggT_ps = pb("aggT_ps", [P, D], fp32)
        selfT_ps = pb("selfT_ps", [P, D], fp32)
        prod_ps = pb("prod_ps", [P, PR * D], fp32)
        hist_ps = pb("hist_ps", [P, D], fp32)
        tmp_ps = [prod_ps[:, n * D:(n + 1) * D] for n in range(3)]

        names = """edges_copied pad_made dst_loaded x_loaded consts_made oh_ready oh_used hist_done deg_made
            total_ps sched_ready rows_gathered tabs_ps tabs_read tabs_made loads_done tbc_made bias_ps bias_made
            staged stage_stored0 stage_stored1 zero_stored w_loaded chain raw_done gathered hi_ready onehot_ready
            pe_done self_loaded self_read selfT_ready agg_ready aggT_done aggT_ready prod_ready prod_read sum_chain
            stats_ready root_ready rstd_ready norm_ready x_stored h_stored h_ready idx_copied
            out_stored flags_ps stats_made slot_claimed x_tail_zero""".split()
        S = {n: sem(n) for n in names}
        slot_full = [sem(f"slot_full{n}") for n in range(SLOTS)]

        block = ctx.enter_context(nc.Block())

        X2 = X[:, :, :].rearrange("p t d -> p (t d)")
        raw2 = raw[:, :, :].rearrange("p n d -> p (n d)")

        def tile_of_x(t1):
            return X2[:, bass.ds(t1 * D - D, D)]

        def raw_slot(b, r):
            return raw2[:, bass.ds((b % (SLOTS // HR)) * (HR * CH * D) + r * CH * D, CH * D)].rearrange("p (j d) -> p j d", j=CH)

        def product(t1):
            return prod_ps[:, bass.ds((t1 % PR) * D, D)]

        def ended_by(eng, w):
            return eng.value_load(ended[0:1, bass.ds(w + WPAD, 1)], min_val=0, max_val=T)

        def each(eng, first, end, part):
            with eng.If(end > first):
                with eng.Fori(first, end) as t:
                    part(nc.s_assert_within(t + 1, 1, T, skip_runtime_bounds_check_because="a tile of the graph"))
                eng.nop()

        @block.sync
        def _(sp):
            full = E // GROUP * GROUP
            for rows, edges in ((src_rows, src), (dst_rows, dst)):
                flat = rows.rearrange("g e -> (g e)")
                sp.dma_start(flat[0:full].rearrange("(g e) -> g e", e=GROUP),
                             edges[0:full].rearrange("(g e) -> g e", e=GROUP)).then_inc(S["edges_copied"], 16)
                sp.dma_start(flat[full:E].rearrange("(a e) -> a e", a=1),
                             edges[full:E].rearrange("(a e) -> a e", a=1)).then_inc(S["edges_copied"], 16)
                if rows is src_rows:
                    sp.wait_ge(S["pad_made"], 1)
                sp.dma_start(flat[E:EPAD].rearrange("(a e) -> a e", a=1),
                             hpad[0:1, 0:EPAD - E]).then_inc(S["edges_copied"], 16)
            sp.wait_ge(S["edges_copied"], 6 * 16)
            flat = dst_rows.rearrange("g e -> (g e)")
            sp.dma_start(dst_nat[:, :], flat[0:P * EC].rearrange("(p c) -> p c", p=P)).then_inc(S["dst_loaded"], 16)
            sp.wait_ge(S["x_tail_zero"], 1)
            sp.dma_start(X[0:TAIL, T - 1, :], x[(T - 1) * P:N, :]).then_inc(S["x_loaded"], 16)
            for a in range(0, T - 1, 8):
                sp.dma_start(X[:, a:a + 8, :],
                             x[a * P:(a + 8) * P, :].rearrange("(t p) d -> p t d", p=P)).then_inc(S["x_loaded"], 16)
            sp.wait_ge(S["hist_done"], 1)
            for p0, row in ((0, b0), (1, bt), (32, b1), (64, b2)):
                sp.dma_start(brow[p0:p0 + 1, :], row.rearrange("(a d) -> a d", a=1)).then_inc(S["loads_done"], 16)
            for k in range(KE):
                sp.dma_start(tcol[:, k:k + 1],
                             t_emb[k * P:(k + 1) * P].rearrange("(p a) -> p a", a=1)).then_inc(S["loads_done"], 16)
            sp.dma_start(late_wt[:, :, :], wt.rearrange("(k p) d -> p k d", p=P)).then_inc(S["loads_done"], 16)
            for L in range(NL):
                if L == 0:
                    sp.wait_ge(S["tabs_made"], 1)
                    sp.wait_ge(S["bias_made"], 1)
                    sp.wait_ge(S["stage_stored0"], 16 * 4)
                    sp.wait_ge(S["stage_stored1"], 16 * 3)
                    sp.dma_start(W[:, 0, :, :], w0.rearrange("(k p) d -> p k d", p=P)).then_inc(S["w_loaded"], 16)
                else:
                    sp.wait_ge(S["prod_ready"], T * L)
                    for n, w in enumerate(((wl1t, wr1t), (wl2t, wr2t))[L - 1]):
                        sp.dma_start(W[:, n, :, :],
                                     w.rearrange("(k p) d -> p k d", p=P)).then_inc(S["w_loaded"], 16)
                with sp.Fori(0, NS, SLOTS) as s:
                    for n in range(SLOTS):
                        sp.wait_ge(slot_full[n], s * (16 * CH // SLOTS) + 16 * CH * (NS // SLOTS * L + 1))
                        sp.sem_inc(S["gathered"], 1)

        @block.gpsimd
        def _(pool):
            nc.gpsimd.memset(hpad[0:1, :], -1).then_inc(S["pad_made"], 1)
            nc.gpsimd.memset(X[:, T - 1, :], 0.0).then_inc(S["x_tail_zero"], 1)
            nc.gpsimd.iota(iota_lo[:, :, :], [[1, P], [0, HB]], base=0, channel_multiplier=0,
                           allow_small_or_imprecise_dtypes=True)
            nc.gpsimd.memset(zeros[:, :], 0.0)
            nc.gpsimd.memset(ended[0:1, 0:WPAD], 0)
            nc.gpsimd.memset(eps[:, :], EPS)
            nc.gpsimd.memset(ident[:, :], 0.0)
            nc.gpsimd.iota(iota_row[:, :], [[1, P]], base=0, channel_multiplier=0,
                           allow_small_or_imprecise_dtypes=True).then_inc(S["consts_made"], 1)
            pool.wait_ge(S["consts_made"], 1)
            nc.gpsimd.affine_select(out=ident[:, :], in_=ident[:, :], compare_op=ALU.not_equal, fill=1.0, base=0,
                                    pattern=[[-1, P]], channel_multiplier=1).then_inc(S["consts_made"], 1)
            pool.wait_ge(S["hist_done"], 1)
            nc.gpsimd.memset(ones[:, :], 1.0)
            nc.gpsimd.iota(iota_t[:, :], [[1, T + 1]], base=0, channel_multiplier=0,
                           allow_small_or_imprecise_dtypes=True)
            nc.gpsimd.iota(iota_s[:, :], [[P, SB]], base=0, channel_multiplier=1,
                           allow_small_or_imprecise_dtypes=True).then_inc(S["consts_made"], 1)
            nc.gpsimd.memset(raw[:, :, :], 0.0).then_inc(S["raw_done"], SLOTS)
            pool.wait_ge(S["sched_ready"], 1)
            for q in range(SB):
                for rows, buf in ((src_rows, srow), (dst_rows, drow)):
                    nc.gpsimd.indirect_dma_start(
                        out=buf[:, q, :], out_offset=None, in_=rows[:, :],
                        in_offset=bass.IndirectOffsetOnAxis(ap=grp_si[:, q:q + 1], axis=0),
                    ).then_inc(S["rows_gathered"], 16)
            pool.wait_ge(S["tabs_made"], 1)
            pool.wait_ge(S["zero_stored"], 16 * NL)
            last_row = pool.to_reg(N - 1)
            for L in range(NL):
                if L == 0:
                    pool.wait_ge(S["stage_stored0"], 16 * 4)
                    pool.wait_ge(S["stage_stored1"], 16 * 3)
                elif L == 1:
                    pool.wait_ge(S["x_stored"], 16 * T)
                else:
                    pool.wait_ge(S["h_stored"], 16 * (T + 1))
                def gather(s, half):
                    nc.gpsimd.tensor_copy(idx_ring[:, half, :, :],
                                          idx_tab[:, :, bass.ds(s, SLOTS)]).then_inc(S["idx_copied"], SLOTS)
                    pool.wait_ge(S["idx_copied"], s + (NS * L + SLOTS))
                    for n in range(SLOTS):
                        pool.wait_ge(S["raw_done"], s + (NS * L + n + 1))
                        pool.sem_inc(S["slot_claimed"], 1)
                        for j in range(CH):
                            nc.gpsimd.indirect_dma_start(
                                out=raw[:, n, j * D:(j + 1) * D], out_offset=None, in_=tables[L][:, :],
                                in_offset=bass.IndirectOffsetOnAxis(ap=idx_ring[:, half, j, n:n + 1], axis=0),
                                bounds_check=last_row, oob_is_err=False,
                            ).then_inc(slot_full[n], 16)

                first = L * (NS // SLOTS) % 2
                pairs = NS // (2 * SLOTS)
                with pool.Fori(0, pairs * 2 * SLOTS, 2 * SLOTS) as s:
                    gather(s, first)
                    gather(s + SLOTS, 1 - first)
                if NS // SLOTS % 2:
                    gather(pairs * 2 * SLOTS, first)

        @block.vector
        def _(dve):
            v = nc.vector
            count = [0]

            def link(ins):
                count[0] += 1
                ins.then_inc(S["chain"], 1)
                dve.wait_ge(S["chain"], count[0])

            dve.sem_inc(S["prod_read"], PR)
            dve.sem_inc(S["sum_chain"], 1)
            dve.sem_inc(S["norm_ready"], 1)
            dve.wait_ge(S["dst_loaded"], 16)
            v.tensor_scalar(dst_hi_i[:, :], dst_nat[:, :], 7, None, ALU.arith_shift_right)
            link(v.tensor_scalar(dst_lo_i[:, :], dst_nat[:, :], P - 1, None, ALU.bitwise_and))
            v.tensor_copy(dst_hi[:, :], dst_hi_i[:, :])
            link(v.tensor_copy(dst_lo[:, :], dst_lo_i[:, :]))
            dve.wait_ge(S["consts_made"], 1)
            with dve.Fori(0, EC // HB) as b:
                dve.wait_ge(S["oh_used"], b + 1)
                lo_b = dst_lo[:, bass.ds(b * HB, HB)].unsqueeze(1).to_broadcast([P, P, HB])
                hi_b = dst_hi[:, bass.ds(b * HB, HB)].unsqueeze(1).to_broadcast([P, T, HB])
                v.tensor_tensor(oh_lo[:, bass.ds((b % 2) * (P * HB), P * HB)].rearrange("p (a c) -> p a c", c=HB),
                                iota_lo[:, :, :], lo_b, ALU.is_equal)
                v.tensor_tensor(oh_hi[:, bass.ds((b % 2) * (T * HB), T * HB)].rearrange("p (a c) -> p a c", c=HB),
                                iota_lo[:, 0:T, :], hi_b, ALU.is_equal).then_inc(S["oh_ready"], 1)
            dve.wait_ge(S["hist_done"], 1)
            dve.wait_ge(S["consts_made"], 3)
            link(v.tensor_copy(cnt[:, :], hist_ps[:, 0:T]))
            link(v.tensor_scalar(rcnt[:, :], cnt[:, :], 1.0, None, ALU.max))
            v.tensor_scalar(dinv[:, :], cnt[:, :], 1.0, None, ALU.add).then_inc(S["deg_made"], 1)
            link(v.reciprocal(rcnt[:, :], rcnt[:, :]))
            dve.wait_ge(S["deg_made"], 2)
            v.reciprocal(dinv[:, :], dinv[:, :]).then_inc(S["deg_made"], 1)
            dve.wait_ge(S["total_ps"], 1)
            link(v.tensor_copy(n_t[:, :], tmp_ps[0][:, 0:T]))
            link(v.tensor_tensor_scan(end_t[:, :], ones[:, 0:T], n_t[:, :], 0.0, ALU.mult, ALU.add))
            v.tensor_tensor(grp_f[:, 0, :], end_t[:, :], n_t[:, :], ALU.subtract)
            link(v.tensor_scalar(grp_f[:, 1, :], end_t[:, :], -1.0, None, ALU.add))
            link(v.tensor_copy(grp_i[:, :, :], grp_f[:, :, :]))
            link(v.tensor_scalar(grp_s[:, :, :], grp_i[:, :, :], 8, None, ALU.arith_shift_right))
            link(v.tensor_copy(grp_f[:, :, :], grp_s[:, :, :]))
            link(v.tensor_tensor(steps_t[:, :], grp_f[:, 1, :], grp_f[:, 0, :], ALU.subtract))
            link(v.tensor_scalar(steps_t[:, :], steps_t[:, :], 1.0, 1.0, ALU.add, ALU.max))
            link(v.tensor_tensor_scan(send_t[:, :], ones[:, 0:T], steps_t[:, :], 0.0, ALU.mult, ALU.add))
            link(v.tensor_tensor(shift_t[:, :], grp_f[:, 0, :], send_t[:, :], ALU.subtract))
            v.tensor_tensor(shift_t[:, :], shift_t[:, :], steps_t[:, :], ALU.add)
            v.tensor_scalar(win_end[:, :], iota_s[:, 0:1], float(HR), float(HR), ALU.mult, ALU.add)
            link(v.tensor_scalar(next_s[:, :], iota_s[:, :], 1.0, None, ALU.add))
            v.tensor_scalar(pick[:, 2, 0, :], send_t[:, :], win_end[:, :], 0.0, ALU.is_le, ALU.add,
                            accum_out=ended_w[:, :])
            for q in range(SB):
                v.tensor_scalar(pick[:, 0, q, 0:T - 1], send_t[:, 0:T - 1], iota_s[:, q:q + 1], 0.0, ALU.is_le,
                                ALU.add, accum_out=tile_s[:, q:q + 1])
                last = v.scalar_tensor_tensor(pick[:, 1, q, :], send_t[:, :], next_s[:, q:q + 1], iota_t[:, 1:T + 1],
                                              ALU.is_equal, ALU.mult, accum_out=flag_s[:, q:q + 1])
            link(last)
            for q in range(SB):
                last = v.scalar_tensor_tensor(pick[:, 2, q, :], iota_t[:, 0:T], tile_s[:, q:q + 1], shift_t[:, :],
                                              ALU.is_equal, ALU.mult, accum_out=base_s[:, q:q + 1])
            link(last)
            link(v.tensor_tensor(grp_sf[:, :], base_s[:, :], iota_s[:, :], ALU.add))
            link(v.tensor_scalar(grp_sf[:, :], grp_sf[:, :], float(NG), 0.0, ALU.min, ALU.max))
            v.tensor_scalar(tile_s[:, :], tile_s[:, :], float(P), None, ALU.mult)
            v.tensor_copy(grp_si[:, :], grp_sf[:, :]).then_inc(S["sched_ready"], 1)
            dve.wait_ge(S["loads_done"], 16 * (5 + KE))
            v.tensor_copy(tbc[:, :, :], tcol[:, :].unsqueeze(2).to_broadcast([P, KE, P])).then_inc(S["tbc_made"], 1)
            dve.wait_ge(S["bias_ps"], 1)
            for n in range(NL):
                last = v.tensor_copy(bias[:, n, :], tmp_ps[n][:, :])
            last.then_inc(S["bias_made"], 1)
            dve.wait_ge(S["rows_gathered"], 16 * 2 * SB)
            for q in range(SB):
                last = v.tensor_scalar(locf[:, q, :], drow[:, q, :], tile_s[:, q:q + 1], None, ALU.subtract)
            link(last)
            v.tensor_scalar(off_lo[:, :, :], locf[:, :, :], 0.0, SKIP, ALU.is_lt, ALU.mult)
            link(v.tensor_scalar(idxf[:, :, :], locf[:, :, :], float(P - 1), SKIP, ALU.is_gt, ALU.mult))
            link(v.tensor_tensor(idxf[:, :, :], idxf[:, :, :], off_lo[:, :, :], ALU.add))
            link(v.tensor_tensor(idxf[:, :, :], idxf[:, :, :], srow[:, :, :], ALU.add))
            v.tensor_scalar(idxf[:, :, :], idxf[:, :, :], SKIP, None, ALU.min)
            v.tensor_scalar(locf[:, :, :], locf[:, :, :], -1.0, float(P), ALU.max, ALU.min).then_inc(S["tabs_ps"], 1)
            for j in range(CH):
                dve.wait_ge(S["tabs_ps"], 2 + j)
                v.tensor_copy(idx_tab[:, j, :], tmp_ps[0][:, :])
                v.tensor_copy(loc_tab[:, j, :], tmp_ps[1][:, :]).then_inc(S["tabs_read"], 1)
            dve.wait_ge(S["flags_ps"], 1)
            v.tensor_copy(flags[0:1, :], tmp_ps[2][0:1, :])
            v.tensor_copy(ended[0:1, WPAD:WPAD + P], hist_ps[0:1, 0:P]).then_inc(S["tabs_made"], 1)
            dve.wait_ge(S["tabs_made"], 1)
            dve.wait_ge(S["stage_stored0"], 16 * 4)
            dve.wait_ge(S["stage_stored1"], 16 * 3)

            def norm(L, t1):
                ends = L // 2 * T
                dve.wait_ge(S["root_ready"], t1 + ends)
                v.reciprocal(rstd[:, :], root[:, :]).then_inc(S["rstd_ready"], 1)
                dve.wait_ge(S["rstd_ready"], t1 + ends)
                v.tensor_scalar(tile_of_x(t1), hbuf[:, :], mv[:, 0:1], rstd[:, :], ALU.subtract,
                                ALU.mult).then_inc(S["norm_ready"], 1)

            def finish(L, t1):
                dve.wait_ge(S["prod_ready"], t1 + T * L)
                if L == 1:
                    dve.wait_ge(S["h_stored"], t1 * 16)
                    v.tensor_tensor(hbuf[:, :], product(t1), bias[:, 1, :], ALU.add).then_inc(S["prod_read"], 1)
                    return
                ends = L // 2 * T
                dve.wait_ge(S["norm_ready"], t1 + ends)
                v.tensor_tensor(hbuf[:, :], product(t1), tile_of_x(t1), ALU.add).then_inc(S["prod_read"], 1)
                dve.wait_ge(S["prod_read"], t1 + (T * L + PR))
                v.tensor_tensor(hbuf[:, :], hbuf[:, :], bias[:, L, :], ALU.add).then_inc(S["sum_chain"], 1)
                dve.wait_ge(S["sum_chain"], t1 * 2 + 2 * ends)
                v.bn_stats(stats[:, :], hbuf[:, :]).then_inc(S["sum_chain"], 1)
                dve.wait_ge(S["sum_chain"], t1 * 2 + (2 * ends + 1))
                dve.sem_inc(S["stats_made"], 1)
                v.bn_aggr(mv[:, :], stats[:, :]).then_inc(S["stats_ready"], 1)

            for L in range(NL):
                def finish_window(b):
                    def part(t1):
                        finish(L, t1)
                        if L != 1:
                            norm(L, t1)

                    each(dve, ended_by(dve, b - 2), ended_by(dve, b - 1), part)

                with dve.Fori(0, NS // HR) as b:
                    s = b * HR
                    for r in range(HR):
                        step = s + (NS * L + r + 1)
                        dve.wait_ge(S["pe_done"], step)
                        for j in range(CH):
                            last = v.tensor_scalar(oh[:, r, j, :], iota_row[:, :],
                                                   loc_tab[:, j, bass.ds(s + r, 1)], None, ALU.is_equal)
                        last.then_inc(S["onehot_ready"], 1)
                        dve.wait_ge(S["hi_ready"], step)
                        v.tensor_tensor(lo[:, r, :, :], raw_slot(b, r), hi[:, r, :, :].bitcast(fp32),
                                        ALU.subtract).then_inc(S["raw_done"], 1)
                    finish_window(b)
                finish_window(NW)

        @block.scalar
        def _(act):
            a = nc.scalar
            act.sem_inc(S["h_stored"], 16)
            act.wait_ge(S["consts_made"], 1)
            act.wait_ge(S["deg_made"], 1)
            a.activation(dinv[:, :], dinv[:, :], ACT.Sqrt).then_inc(S["deg_made"], 1)
            act.wait_ge(S["deg_made"], 3)
            act.wait_ge(S["x_loaded"], 16 * (1 + (T - 1) // 8))
            stored = (S["stage_stored0"], S["stage_stored1"])
            for b in range(NB):
                if b >= 2:
                    act.wait_ge(stored[b % 2], 16 * (b // 2))
                for k in range(BT):
                    t = b * BT + k
                    last = a.activation(stage[:, b % 2, k, :], X[:, t, :], ACT.Copy, scale=dinv[:, t:t + 1])
                last.then_inc(S["staged"], 1)
                act.wait_ge(S["staged"], b + 1)
                act.dma_start(tables[0][b * BT * P:(b + 1) * BT * P, :].rearrange("(t p) d -> p t d", p=P),
                              stage[:, b % 2, :, :]).then_inc(stored[b % 2], 16)
            act.wait_ge(S["raw_done"], SLOTS)
            for n in range(NL):
                act.dma_start(tables[n][T * P:(T + 1) * P, :], raw[:, 0, 0:D]).then_inc(S["zero_stored"], 16)
            act.wait_ge(S["zero_stored"], 16 * NL)
            act.wait_ge(S["tabs_made"], 1)
            act.wait_ge(S["bias_made"], 1)
            act.wait_ge(S["stage_stored0"], 16 * 4)
            act.wait_ge(S["stage_stored1"], 16 * 3)

            def flush(L, t1):
                scale = (dinv, rcnt, rcnt)[L]
                act.wait_ge(S["self_read"], t1 + T * L)
                a.activation(agg[:, :], sum_ps[:, :], ACT.Copy,
                             scale=scale[:, bass.ds(t1 - 1, 1)]).then_inc(S["agg_ready"], 1)
                act.dma_start(selfbuf[:, :], tables[L][bass.ds(t1 * P, P), :]).then_inc(S["self_loaded"], 16)
                if L > 0:
                    a.activation(selfT[:, :], selfT_ps[:, :], ACT.Copy).then_inc(S["selfT_ready"], 1)
                act.wait_ge(S["aggT_done"], t1 + T * L)
                a.activation(aggT[:, :], aggT_ps[:, :], ACT.Copy).then_inc(S["aggT_ready"], 1)

            def square_root(L, t1):
                ends = L // 2 * T
                if L == 1:
                    act.wait_ge(S["prod_read"], t1 + (T * L + PR))
                    a.activation(hbuf[:, :], hbuf[:, :], ACT.Relu).then_inc(S["h_ready"], 1)
                    act.wait_ge(S["h_ready"], t1)
                    act.dma_start(tables[2][bass.ds(t1 * P - P, P), :], hbuf[:, :]).then_inc(S["h_stored"], 16)
                    return
                act.wait_ge(S["stats_ready"], t1 + ends)
                a.activation(root[:, :], mv[:, 1:2], ACT.Sqrt,
                             bias=eps[:, 0:1]).then_inc(S["root_ready"], 1)

            def store(L, t1):
                act.wait_ge(S["norm_ready"], t1 + (L // 2 * T + 1))
                if L == 0:
                    act.dma_start(tables[1][bass.ds(t1 * P - P, P), :], tile_of_x(t1)).then_inc(S["x_stored"], 16)
                else:
                    with act.If(t1 < T):
                        full = nc.s_assert_within(t1, 1, T - 1, skip_runtime_bounds_check_because="not the last tile")
                        act.dma_start(out[bass.ds(full * P - P, P), :], tile_of_x(full)).then_inc(S["out_stored"], 16)
                    act.nop()

            for L in range(NL):
                def after_steps(b):
                    e = [ended_by(act, b - k) for k in (3, 2, 1, 0)]
                    if L != 1:
                        each(act, e[0], e[1], lambda t1: store(L, t1))
                    each(act, e[1], e[2], lambda t1: square_root(L, t1))
                    each(act, e[2], e[3], lambda t1: flush(L, t1))

                if L == 1:
                    act.wait_ge(S["x_stored"], 16 * T)
                elif L == 2:
                    act.wait_ge(S["h_stored"], 16 * (T + 1))
                if L > 0:
                    act.wait_ge(S["self_loaded"], 16 * (T + 1) * L)
                act.dma_start(selfbuf[:, :], tables[L][0:P, :]).then_inc(S["self_loaded"], 16)
                with act.Fori(0, NS // HR) as b:
                    s = b * HR
                    for r in range(HR):
                        step = s + (NS * L + r + 1)
                        act.wait_ge(S["gathered"], step)
                        act.wait_ge(S["pe_done"], step)
                        a.activation(hi[:, r, :, :], raw_slot(b, r), ACT.Copy).then_inc(S["hi_ready"], 1)
                    after_steps(b)
                after_steps(NW)
                after_steps(NW + 1)
            act.wait_ge(S["norm_ready"], 2 * T + 1)
            act.dma_start(out[(T - 1) * P:N, :], X[0:TAIL, T - 1, :]).then_inc(S["out_stored"], 16)
            act.wait_ge(S["out_stored"], 16 * T)
            act.wait_ge(S["self_loaded"], 16 * (T + 1) * NL)

        @block.tensor
        def _(pe):
            mm = nc.tensor.matmul

            def clear(bank, cols, n=1):
                return mm(bank[:, 0:cols], zeros[:, :], zeros[:, 0:1].to_broadcast([P, cols]), start=True, stop=False,
                          skip_group_check=True)

            pe.sem_inc(S["oh_used"], 2)
            pe.sem_inc(S["pe_done"], HR)
            pe.wait_ge(S["consts_made"], 2)
            clear(hist_ps, T)
            with pe.Fori(0, EC // HB) as b:
                pe.wait_ge(S["oh_ready"], b + 1)
                lo_b = oh_lo[:, bass.ds((b % 2) * (P * HB), P * HB)].rearrange("p (a c) -> p a c", c=HB)
                hi_b = oh_hi[:, bass.ds((b % 2) * (T * HB), T * HB)].rearrange("p (a c) -> p a c", c=HB)
                for c in range(HB):
                    last = mm(hist_ps[:, 0:T], lo_b[:, :, c], hi_b[:, :, c], start=False, stop=False,
                              skip_group_check=True)
                last.then_inc(S["oh_used"], 1)
            mm(hist_ps[:, 0:T], zeros[:, :], zeros[:, 0:T], start=False, stop=True,
               skip_group_check=True).then_inc(S["hist_done"], 1)
            pe.wait_ge(S["consts_made"], 3)
            pe.wait_ge(S["deg_made"], 1)
            mm(tmp_ps[0][:, 0:T], ones[:, :], cnt[:, :], start=True, stop=True).then_inc(S["total_ps"], 1)
            pe.wait_ge(S["tbc_made"], 1)
            for k in range(KE):
                mm(tmp_ps[0][:, :], tbc[:, k, :], late_wt[:, k, :], start=(k == 0), stop=False)
            mm(tmp_ps[0][:, :], ones[0:2, :], brow[0:2, :], start=False, stop=True)
            mm(tmp_ps[1][:, :], ones[32:33, :], brow[32:33, :], start=True, stop=True)
            mm(tmp_ps[2][:, :], ones[64:65, :], brow[64:65, :], start=True, stop=True).then_inc(S["bias_ps"], 1)
            pe.wait_ge(S["bias_made"], 1)
            pe.wait_ge(S["tabs_ps"], 1)
            for q in range(SB):
                nc.tensor.transpose(tmp_ps[2][0:1, q * P:(q + 1) * P], flag_s[:, q:q + 1], ident[:, :])
            last = nc.tensor.transpose(hist_ps[0:1, 0:P], ended_w[:, :], ident[:, :])
            last.then_inc(S["flags_ps"], 1)
            for j in range(CH):
                if j > 0:
                    pe.wait_ge(S["tabs_read"], j)
                for q in range(SB):
                    nc.tensor.transpose(tmp_ps[0][:, q * P:(q + 1) * P], idxf[:, q, j * P:(j + 1) * P], ident[:, :])
                for q in range(SB):
                    last = nc.tensor.transpose(tmp_ps[1][:, q * P:(q + 1) * P], locf[:, q, j * P:(j + 1) * P],
                                               ident[:, :])
                last.then_inc(S["tabs_ps"], 1)
            pe.wait_ge(S["tabs_made"], 1)

            def flush(L, t1):
                tile = t1 + T * L
                pe.wait_ge(S["self_loaded"], (t1 + (T + 1) * L) * 16)
                if L == 0:
                    mm(sum_ps[:, :], ident[:, :], selfbuf[:, :], start=False, stop=True,
                       skip_group_check=True).then_inc(S["self_read"], 1)
                else:
                    for k in range(KD):
                        last = nc.tensor.transpose(selfT_ps[:, k * P:(k + 1) * P], selfbuf[:, k * P:(k + 1) * P],
                                                   ident[:, :])
                    last.then_inc(S["self_read"], 1)
                pe.wait_ge(S["agg_ready"], tile)
                for k in range(KD):
                    last = nc.tensor.transpose(aggT_ps[:, k * P:(k + 1) * P], agg[:, k * P:(k + 1) * P], ident[:, :])
                last.then_inc(S["aggT_done"], 1)
                clear(sum_ps, D)
                pe.wait_ge(S["prod_read"], tile)
                if L > 0:
                    pe.wait_ge(S["selfT_ready"], t1 + T * (L - 1))
                    for k in range(KD):
                        mm(product(t1), selfT[:, k * P:(k + 1) * P], W[:, 1, k, :], start=(k == 0), stop=False)
                pe.wait_ge(S["aggT_ready"], tile)
                for k in range(KD):
                    last = mm(product(t1), aggT[:, k * P:(k + 1) * P], W[:, 0, k, :], start=(L == 0 and k == 0),
                              stop=(k == KD - 1))
                last.then_inc(S["prod_ready"], 1)

            clear(sum_ps, D)
            for L in range(NL):
                pe.wait_ge(S["w_loaded"], 16 * (1 + 2 * L))
                with pe.Fori(0, NS // HR) as b:
                    s = b * HR
                    last_of = [pe.value_load(flags[0:1, bass.ds(s + r, 1)], min_val=0, max_val=T) for r in range(HR)]
                    for r in range(HR):
                        step = s + (NS * L + r + 1)
                        pe.wait_ge(S["onehot_ready"], step)
                        pe.wait_ge(S["hi_ready"], step)
                        for j in range(CH):
                            mm(sum_ps[:, :], oh[:, r, j, :], hi[:, r, j, :], start=False, stop=False,
                               skip_group_check=True)
                        pe.wait_ge(S["raw_done"], step + SLOTS)
                        for j in range(CH):
                            last = mm(sum_ps[:, :], oh[:, r, j, :], lo[:, r, j, :], start=False, stop=False,
                                      skip_group_check=True)
                        last.then_inc(S["pe_done"], 1)
                        with pe.If(last_of[r] > 0):
                            flush(L, nc.s_assert_within(last_of[r], 1, T,
                                                        skip_runtime_bounds_check_because="the flag is not zero here"))


_INS = ['x', 'src', 'dst', 'L0_gnn_t_emb', 'L0_gnn_W', 'L0_gnn_b', 'L0_gnn_Wt', 'L0_gnn_bt', 'L1_gnn_Wl1', 'L1_gnn_Wr1',
        'L1_gnn_b1', 'L1_gnn_Wl2', 'L1_gnn_Wr2', 'L1_gnn_b2']
_TRANSPOSED = ('L1_gnn_Wl1', 'L1_gnn_Wr1', 'L1_gnn_Wl2', 'L1_gnn_Wr2')


def build(nc, arrays):
    args = [nc.dram_tensor(f"in_{n}", arrays[f"in_{n}"].shape, mybir.dt.from_np(arrays[f"in_{n}"].dtype),
                           kind="ExternalInput").ap() for n in _INS]
    out = nc.dram_tensor("out_0", arrays["in_x"].shape, mybir.dt.float32, kind="ExternalOutput").ap()
    gnn_resnorm(nc, *args, out)


def kernel(**inputs):
    import numpy as np
    import concourse.bacc as bacc
    from concourse.bass_utils import run_bass_kernel_spmd

    nc = bacc.Bacc("TRN2", target_bir_lowering=False, num_devices=1)
    arrays = {}
    for n in _INS:
        w = np.asarray(inputs[n])
        arrays[f"in_{n}"] = np.ascontiguousarray(w.T if n in _TRANSPOSED else w)
    build(nc, arrays)
    return run_bass_kernel_spmd(nc, [arrays], core_ids=[0]).results[0]["out_0"]
```

```python
import concourse.bass as bass
from concourse import mybir
from contextlib import ExitStack


def gnn_resnorm(nc, x, src, dst, t_emb, w0, b0, wt, bt, wl1t, wr1t, b1, wl2t, wr2t, b2, out):
    fp32, f32r, bf16 = mybir.dt.float32, mybir.dt.float32r, mybir.dt.bfloat16
    i32, u16 = mybir.dt.int32, mybir.dt.uint16
    ALU, ACT = mybir.AluOpType, mybir.ActivationFunctionType

    N, D = x.shape
    E = src.shape[0]
    P = 128
    T = -(-N // P)
    TAIL = N - (T - 1) * P
    KD = D // P
    KE = t_emb.shape[0] // P
    EPS = 1e-5

    CH = 2
    GROUP = CH * P
    NG = -(-E // GROUP)
    SLOTS = 8
    HR = 4
    NS = -(-(NG + T - 1) // SLOTS) * SLOTS
    NW = NS // HR
    SB = -(-NS // P)
    PR = 4
    LEAD = 3
    DEV_LAG = PR + 1
    NORM_LAG = DEV_LAG + 1
    STORE_LAG = DEV_LAG + NORM_LAG + 1
    WPAD = 2
    ROOT_RATE = T / (0.48 * NS / HR)
    SKIP = 65535.0
    NL = 3
    EC = -(-E // P)
    HB = 34
    EPAD = (NG + 1) * GROUP
    NB, BT = 7, T // 7
    assert EC % HB == 0 and NB * BT == T and NS % SLOTS == 0 and SLOTS % HR == 0 and EC // HB % 2 == 1

    ctx = ExitStack()
    with ctx:
        def sb(name, shape, dt, scope=ctx):
            return scope.enter_context(nc.sbuf_tensor(name, shape, dt))

        def pb(name, shape, dt):
            return ctx.enter_context(nc.psum_tensor(name, shape, dt))

        def sem(name):
            return ctx.enter_context(nc.semaphore(name))

        src_rows = nc.dram_tensor("src_rows", [NG + 1, GROUP], i32, kind="Internal").ap()
        dst_rows = nc.dram_tensor("dst_rows", [NG + 1, GROUP], i32, kind="Internal").ap()
        tables = [nc.dram_tensor(f"table{n}", [(T + 2) * P, D], fp32, kind="Internal").ap() for n in range(NL)]

        X = sb("X", [P, T, D], fp32)
        idx_tab = sb("idx_tab", [P, CH, SB * P], u16)
        loc_tab = sb("loc_tab", [P, CH, SB * P], bf16)
        flags = sb("flags", [1, SB * P], i32)
        ended = sb("ended", [1, WPAD + P], i32)
        rooted = sb("rooted", [1, WPAD + P], i32)
        brow = sb("brow", [P, D], f32r)
        ones = sb("ones", [P, P], fp32)
        ident = sb("ident", [P, P], fp32)
        iota_row = sb("iota_row", [P, P], bf16)
        zeros = sb("zeros", [P, P], bf16)
        dinv = sb("dinv", [P, T], fp32)
        rcnt = sb("rcnt", [P, T], fp32)
        sums = sb("sums", [P, T], fp32)
        root = sb("root", [P, T], fp32)
        sqsum = sb("sqsum", [P, T], fp32)
        eps = sb("eps", [P, 1], fp32)
        unsorted = sb("unsorted", [1, 8], i32)
        idx_ring = sb("idx_ring", [P, 2, CH, SLOTS], i32)

        early = ExitStack()
        dst_nat = sb("dst_nat", [P, EC], i32, early)
        dst_hi_i = sb("dst_hi_i", [P, EC], i32, early)
        dst_lo_i = sb("dst_lo_i", [P, EC], i32, early)
        dst_hi = sb("dst_hi", [P, EC], bf16, early)
        dst_lo = sb("dst_lo", [P, EC], bf16, early)
        iota_lo = sb("iota_lo", [P, P, HB], bf16, early)
        oh_lo = sb("oh_lo", [P, 2, P, HB], bf16, early)
        oh_hi = sb("oh_hi", [P, 2, T, HB], bf16, early)
        dst_next = sb("dst_next", [P, EC], i32, early)
        next_hi_i = sb("next_hi_i", [P, EC], i32, early)
        next_hi = sb("next_hi", [P, EC], bf16, early)
        falls = sb("falls", [P, EC], bf16, early)
        fall_sum = sb("fall_sum", [P, 1], fp32, early)
        hpad = sb("hpad", [1, EPAD - E], i32, early)
        early.close()

        mid = ExitStack()
        stage = sb("stage", [P, 2, BT, D], fp32, mid)
        srow = sb("srow", [P, SB, GROUP], i32, mid)
        drow = sb("drow", [P, SB, GROUP], i32, mid)
        locf = sb("locf", [P, SB, GROUP], fp32, mid)
        idxf = sb("idxf", [P, SB, GROUP], fp32, mid)
        off_lo = sb("off_lo", [P, SB, GROUP], fp32, mid)
        late_wt = sb("late_wt", [P, KE, D], fp32, mid)
        tcol = sb("tcol", [P, KE, 2], fp32, mid)
        bin_row = sb("bin_row", [P, D], fp32, mid)
        bias_hi = sb("bias_hi", [P, D], fp32, mid)
        bias_lo = sb("bias_lo", [P, D], fp32, mid)
        cnt = sb("cnt", [P, T], fp32, mid)
        n_t = sb("n_t", [P, T], fp32, mid)
        end_t = sb("end_t", [P, T], fp32, mid)
        grp_f = sb("grp_f", [P, 2, T], fp32, mid)
        grp_i = sb("grp_i", [P, 2, T], i32, mid)
        grp_s = sb("grp_s", [P, 2, T], i32, mid)
        steps_t = sb("steps_t", [P, T], fp32, mid)
        send_t = sb("send_t", [P, T], fp32, mid)
        shift_t = sb("shift_t", [P, T], fp32, mid)
        iota_t = sb("iota_t", [P, T + 1], fp32, mid)
        iota_s = sb("iota_s", [P, SB], fp32, mid)
        pick = sb("pick", [P, 3, SB, T], fp32, mid)
        tile_s = sb("tile_s", [P, SB], fp32, mid)
        base_s = sb("base_s", [P, SB], fp32, mid)
        grp_sf = sb("grp_sf", [P, SB], fp32, mid)
        grp_si = sb("grp_si", [P, SB], i32, mid)
        flag_s = sb("flag_s", [P, SB], fp32, mid)
        next_s = sb("next_s", [P, SB], fp32, mid)
        ended_w = sb("ended_w", [P, 1], fp32, mid)
        rooted_w = sb("rooted_w", [P, 2], fp32, mid)
        win_end = sb("win_end", [P, 1], fp32, mid)
        mid.close()

        hi = sb("hi", [P, SLOTS, CH, D], f32r)
        oh = sb("oh", [P, SLOTS, CH, P], f32r)
        W = sb("W", [P, 2, KD, D], fp32)
        selfbuf = sb("selfbuf", [P, D], fp32)
        agg = sb("agg", [P, D], fp32)
        selfT = sb("selfT", [P, D], fp32)
        aggT = sb("aggT", [P, D], fp32)
        hbuf = sb("hbuf", [P, D], fp32)
        sort = ExitStack()
        sort_src = sb("sort_src", [P, EC], i32, sort)
        sort_dst = sb("sort_dst", [P, EC], i32, sort)
        sort_tile_i = sb("sort_tile_i", [P, EC], i32, sort)
        sort_tile = sb("sort_tile", [P, EC], fp32, sort)
        sort_skip = sb("sort_skip", [P, EC], fp32, sort)
        before = sb("before", [P, P], fp32, sort)
        not_before = sb("not_before", [P, P], fp32, sort)
        sort_oh = sb("sort_oh", [P, T], fp32, sort)
        sort_at = sb("sort_at", [P, 2, T], fp32, sort)
        place = sb("place", [P, 1], fp32, sort)
        place_i = sb("place_i", [P, 1], i32, sort)
        edge_val = sb("edge_val", [P, 2], i32, sort)
        sort.close()
        raw = sb("raw", [P, SLOTS, CH, D], fp32)

        sum_ps = pb("sum_ps", [P, D], fp32)
        aggT_ps = pb("aggT_ps", [P, D], fp32)
        selfT_ps = pb("selfT_ps", [P, D], fp32)
        prod_ps = pb("prod_ps", [P, PR * D], fp32)
        root_ps = pb("root_ps", [P, D], fp32)
        hist_ps = root_ps
        tmp_ps = [prod_ps[:, n * D:(n + 1) * D] for n in range(3)]

        names = """edges_copied pad_made dst_loaded x_loaded consts_made oh_ready oh_used hist_done deg_made
            total_ps sched_ready rows_gathered tabs_ps tabs_read tabs_made loads_done bias_ps bias_made
            staged stage_stored0 stage_stored1 zero_stored w_loaded chain lo_ready zeroed gathered hi_ready
            pe_done self_loaded sum_ready agg_ready aggT_done aggT_ready prod_ready prod_read
            selfT_done selfT_ready root_ready root_added root_taken
            mean_ready squares_made rstd_ready norm_ready x_stored h_stored h_ready x_reloaded idx_copied
            out_stored flags_ps slot_claimed x_tail_zero""".split()
        names += """order_read order_known sort_loaded sort_consts sort_oh_made sort_ranked sort_placed
            sort_counted sort_scattered sort_taken sort_read sort_made sort_done""".split()
        S = {n: sem(n) for n in names}
        slot_full = [sem(f"slot_full{n}") for n in range(SLOTS)]

        block = ctx.enter_context(nc.Block())

        X2 = X[:, :, :].rearrange("p t d -> p (t d)")
        lo = raw[:, :, :, :].bitcast(f32r)

        def tile_of_x(t1):
            return X2[:, bass.ds(t1 * D - D, D)]

        def column(per_node, t1):
            return per_node[:, bass.ds(t1 - 1, 1)]

        def product(t1):
            return prod_ps[:, bass.ds((t1 % PR) * D, D)]

        def by_end_of(eng, row, w):
            return eng.value_load(row[0:1, bass.ds(w + WPAD, 1)], min_val=0, max_val=T + 1)

        def lagged(t1, lag):
            return nc.s_assert_within(t1 - lag, 1, T, skip_runtime_bounds_check_because="the first tiles are left out")

        def each(eng, first, end, part, most=T):
            with eng.If(end > first):
                with eng.Fori(first, end) as t:
                    part(nc.s_assert_within(t + 1, 1, most, skip_runtime_bounds_check_because="a tile of the graph"))
                eng.nop()

        @block.sync
        def _(sp):
            full = E // GROUP * GROUP
            for rows, edges in ((src_rows, src), (dst_rows, dst)):
                flat = rows.rearrange("g e -> (g e)")
                sp.dma_start(flat[0:full].rearrange("(g e) -> g e", e=GROUP),
                             edges[0:full].rearrange("(g e) -> g e", e=GROUP)).then_inc(S["edges_copied"], 16)
                sp.dma_start(flat[full:E].rearrange("(a e) -> a e", a=1),
                             edges[full:E].rearrange("(a e) -> a e", a=1)).then_inc(S["edges_copied"], 16)
                if rows is src_rows:
                    sp.wait_ge(S["pad_made"], 1)
                sp.dma_start(flat[E:EPAD].rearrange("(a e) -> a e", a=1),
                             hpad[0:1, 0:EPAD - E]).then_inc(S["edges_copied"], 16)
            sp.wait_ge(S["edges_copied"], 6 * 16)
            flat = dst_rows.rearrange("g e -> (g e)")
            sp.dma_start(dst_nat[:, :], flat[0:P * EC].rearrange("(p c) -> p c", p=P)).then_inc(S["dst_loaded"], 16)
            sp.dma_start(dst_next[:, :],
                         flat[1:P * EC + 1].rearrange("(p c) -> p c", p=P)).then_inc(S["dst_loaded"], 16)
            sp.wait_ge(S["x_tail_zero"], 1)
            sp.dma_start(X[0:TAIL, T - 1, :], x[(T - 1) * P:N, :]).then_inc(S["x_loaded"], 16)
            for a in range(0, T - 1, 8):
                sp.dma_start(X[:, a:a + 8, :],
                             x[a * P:(a + 8) * P, :].rearrange("(t p) d -> p t d", p=P)).then_inc(S["x_loaded"], 16)
            sp.wait_ge(S["hist_done"], 1)
            for p0, row in ((0, b0), (1, bt)):
                sp.dma_start(bin_row[p0:p0 + 1, :], row.rearrange("(a d) -> a d", a=1)).then_inc(S["loads_done"], 16)
            for k in range(KE):
                for row in range(2):
                    sp.dma_start(tcol[:, k, row:row + 1],
                                 t_emb[k * P:(k + 1) * P].rearrange("(p a) -> p a", a=1)).then_inc(S["loads_done"], 16)
            sp.dma_start(late_wt[:, :, :], wt.rearrange("(k p) d -> p k d", p=P)).then_inc(S["loads_done"], 16)
            sp.wait_ge(S["order_known"], 1)
            with sp.If(sp.value_load(unsorted[0:1, 0:1], min_val=0, max_val=EPAD) > 0):
                for rows, buf in ((src_rows, sort_src), (dst_rows, sort_dst)):
                    flat = rows.rearrange("g e -> (g e)")
                    sp.dma_start(buf[:, :],
                                 flat[0:P * EC].rearrange("(p c) -> p c", p=P)).then_inc(S["sort_loaded"], 16)
            sp.nop()
            for L in range(NL):
                if L == 0:
                    sp.wait_ge(S["tabs_made"], 1)
                    sp.wait_ge(S["bias_made"], 1)
                    sp.wait_ge(S["stage_stored0"], 16 * 4)
                    sp.wait_ge(S["stage_stored1"], 16 * 3)
                    sp.dma_start(W[:, 0, :, :], w0.rearrange("(k p) d -> p k d", p=P)).then_inc(S["w_loaded"], 16)
                else:
                    sp.wait_ge(S["prod_ready"], T * L)
                    if L == 2:
                        sp.wait_ge(S["root_ready"], T + 2)
                    for row in range(2):
                        sp.dma_start(agg[row:row + 1, :],
                                     (b1, b2)[L - 1].rearrange("(a d) -> a d", a=1)).then_inc(S["w_loaded"], 16)
                    for n, w in enumerate(((wl1t, wr1t), (wl2t, wr2t))[L - 1]):
                        sp.dma_start(W[:, n, :, :],
                                     w.rearrange("(k p) d -> p k d", p=P)).then_inc(S["w_loaded"], 16)
                with sp.Fori(0, NS, SLOTS) as s:
                    for n in range(SLOTS):
                        sp.wait_ge(slot_full[n], s * (16 * CH // SLOTS) + 16 * CH * (NS // SLOTS * L + 1))
                        sp.sem_inc(S["gathered"], 1)

        @block.gpsimd
        def _(pool):
            nc.gpsimd.memset(hpad[0:1, :], -1).then_inc(S["pad_made"], 1)
            nc.gpsimd.memset(X[:, T - 1, :], 0.0).then_inc(S["x_tail_zero"], 1)
            nc.gpsimd.iota(iota_lo[:, :, :], [[1, P], [0, HB]], base=0, channel_multiplier=0,
                           allow_small_or_imprecise_dtypes=True)
            nc.gpsimd.memset(zeros[:, :], 0.0)
            nc.gpsimd.memset(ones[:, :], 1.0)
            nc.gpsimd.memset(ended[0:1, 0:WPAD], 0)
            nc.gpsimd.memset(rooted[0:1, 0:WPAD], 0)
            nc.gpsimd.memset(eps[:, :], EPS)
            nc.gpsimd.memset(ident[:, :], 0.0)
            nc.gpsimd.iota(iota_row[:, :], [[1, P]], base=0, channel_multiplier=0,
                           allow_small_or_imprecise_dtypes=True).then_inc(S["consts_made"], 1)
            pool.wait_ge(S["consts_made"], 1)
            nc.gpsimd.affine_select(out=ident[:, :], in_=ident[:, :], compare_op=ALU.not_equal, fill=1.0, base=0,
                                    pattern=[[-1, P]], channel_multiplier=1).then_inc(S["consts_made"], 1)
            pool.wait_ge(S["hist_done"], 1)
            nc.gpsimd.iota(iota_t[:, :], [[1, T + 1]], base=0, channel_multiplier=0,
                           allow_small_or_imprecise_dtypes=True)
            nc.gpsimd.iota(iota_s[:, :], [[P, SB]], base=0, channel_multiplier=1,
                           allow_small_or_imprecise_dtypes=True).then_inc(S["consts_made"], 1)
            pool.wait_ge(S["order_known"], 1)
            with pool.If(pool.value_load(unsorted[0:1, 0:1], min_val=0, max_val=EPAD) > 0):
                nc.gpsimd.affine_select(out=before[:, :], in_=ones[:, :], compare_op=ALU.is_gt, fill=0.0, base=0,
                                        pattern=[[1, P]], channel_multiplier=-1)
                nc.gpsimd.affine_select(out=not_before[:, :], in_=ones[:, :], compare_op=ALU.is_ge, fill=0.0, base=0,
                                        pattern=[[-1, P]], channel_multiplier=1).then_inc(S["sort_consts"], 1)
                last_edge = pool.to_reg(E - 1)
                with pool.Fori(0, EC) as c:
                    pool.wait_ge(S["sort_placed"], c + 1)
                    for k, rows in enumerate((src_rows, dst_rows)):
                        pool.sem_inc(S["sort_taken"], 1)
                        nc.gpsimd.indirect_dma_start(
                            out=rows.rearrange("g (e a) -> (g e) a", a=1),
                            out_offset=bass.IndirectOffsetOnAxis(ap=place_i[:, 0:1], axis=0),
                            in_=edge_val[:, k:k + 1], in_offset=None,
                            bounds_check=last_edge, oob_is_err=False).then_inc(S["sort_scattered"], 16)
                pool.wait_ge(S["sort_done"], 2)
            pool.nop()
            nc.gpsimd.memset(raw[:, :, :, :], 0.0).then_inc(S["zeroed"], 1)
            pool.wait_ge(S["sched_ready"], 1)
            for q in range(SB):
                for rows, buf in ((src_rows, srow), (dst_rows, drow)):
                    nc.gpsimd.indirect_dma_start(
                        out=buf[:, q, :], out_offset=None, in_=rows[:, :],
                        in_offset=bass.IndirectOffsetOnAxis(ap=grp_si[:, q:q + 1], axis=0),
                    ).then_inc(S["rows_gathered"], 16)
            pool.wait_ge(S["tabs_made"], 1)
            pool.wait_ge(S["zero_stored"], 16 * NL)
            last_row = pool.to_reg(N - 1)
            for L in range(NL):
                if L == 0:
                    pool.wait_ge(S["stage_stored0"], 16 * 4)
                    pool.wait_ge(S["stage_stored1"], 16 * 3)
                elif L == 1:
                    pool.wait_ge(S["x_stored"], 16 * T)
                else:
                    pool.wait_ge(S["h_stored"], 16 * (T + DEV_LAG + 1))

                def gather(s, half):
                    nc.gpsimd.tensor_copy(idx_ring[:, half, :, :],
                                          idx_tab[:, :, bass.ds(s, SLOTS)]).then_inc(S["idx_copied"], SLOTS)
                    pool.wait_ge(S["idx_copied"], s + (NS * L + SLOTS))
                    for n in range(SLOTS):
                        pool.wait_ge(S["pe_done"], s + (NS * L + n + 1))
                        pool.sem_inc(S["slot_claimed"], 1)
                        for j in range(CH):
                            nc.gpsimd.indirect_dma_start(
                                out=raw[:, n, j, :], out_offset=None, in_=tables[L][:, :],
                                in_offset=bass.IndirectOffsetOnAxis(ap=idx_ring[:, half, j, n:n + 1], axis=0),
                                bounds_check=last_row, oob_is_err=False,
                            ).then_inc(slot_full[n], 16)

                first = L * (NS // SLOTS) % 2
                pairs = NS // (2 * SLOTS)
                with pool.Fori(0, pairs * 2 * SLOTS, 2 * SLOTS) as s:
                    gather(s, first)
                    gather(s + SLOTS, 1 - first)
                if NS // SLOTS % 2:
                    gather(pairs * 2 * SLOTS, first)

        @block.vector
        def _(dve):
            v = nc.vector
            count = [0]

            def link(ins):
                count[0] += 1
                ins.then_inc(S["chain"], 1)
                dve.wait_ge(S["chain"], count[0])

            def split_bias(row, high, low):
                link(v.tensor_copy(high[0:2, :].bitcast(f32r), row[0:2, :]))
                link(v.tensor_tensor(low[0:2, :], row[0:2, :], high[0:2, :], ALU.subtract))
                link(v.tensor_scalar(high[0:2, :], high[0:2, :], ident[0:2, 0:1], None, ALU.mult))
                v.scalar_tensor_tensor(brow[0:2, :], low[0:2, :], ident[0:2, 1:2], high[0:2, :], ALU.mult,
                                       ALU.add).then_inc(S["bias_made"], 1)

            dve.sem_inc(S["prod_read"], PR)
            dve.sem_inc(S["mean_ready"], DEV_LAG)
            dve.sem_inc(S["rstd_ready"], NORM_LAG)
            dve.sem_inc(S["norm_ready"], STORE_LAG)
            dve.wait_ge(S["dst_loaded"], 32)
            v.tensor_scalar(dst_hi_i[:, :], dst_nat[:, :], 7, None, ALU.arith_shift_right)
            link(v.tensor_scalar(dst_lo_i[:, :], dst_nat[:, :], P - 1, None, ALU.bitwise_and))
            v.tensor_copy(dst_hi[:, :], dst_hi_i[:, :])
            v.tensor_scalar(next_hi_i[:, :], dst_next[:, :], 7, None, ALU.arith_shift_right)
            link(v.tensor_copy(dst_lo[:, :], dst_lo_i[:, :]))
            link(v.tensor_copy(next_hi[:, :], next_hi_i[:, :]))
            link(v.tensor_tensor(falls[:, :], dst_hi[:, :], next_hi[:, :], ALU.is_gt))
            v.scalar_tensor_tensor(falls[:, :], next_hi[:, :], 0.0, falls[:, :], ALU.is_ge, ALU.mult,
                                   accum_out=fall_sum[:, :]).then_inc(S["order_read"], 1)
            dve.wait_ge(S["consts_made"], 1)
            def one_hots(b, half):
                dve.wait_ge(S["oh_used"], b + 1)
                lo_b = dst_lo[:, bass.ds(b * HB, HB)].unsqueeze(1).to_broadcast([P, P, HB])
                hi_b = dst_hi[:, bass.ds(b * HB, HB)].unsqueeze(1).to_broadcast([P, T, HB])
                v.tensor_tensor(oh_lo[:, half, :, :], iota_lo[:, :, :], lo_b, ALU.is_equal)
                v.tensor_tensor(oh_hi[:, half, :, :], iota_lo[:, 0:T, :], hi_b,
                                ALU.is_equal).then_inc(S["oh_ready"], 1)

            with dve.Fori(0, EC // HB - 1, 2) as b:
                one_hots(b, 0)
                one_hots(b + 1, 1)
            one_hots(EC // HB - 1, 0)
            dve.wait_ge(S["hist_done"], 1)
            v.tensor_copy(unsorted[0:1, 0:1], aggT_ps[0:1, 0:1]).then_inc(S["order_known"], 1)
            dve.wait_ge(S["consts_made"], 3)
            link(v.tensor_copy(cnt[:, :], hist_ps[:, 0:T]))
            link(v.tensor_scalar(rcnt[:, :], cnt[:, :], 1.0, None, ALU.max))
            v.tensor_scalar(dinv[:, :], cnt[:, :], 1.0, None, ALU.add).then_inc(S["deg_made"], 1)
            link(v.reciprocal(rcnt[:, :], rcnt[:, :]))
            dve.wait_ge(S["deg_made"], 2)
            v.reciprocal(dinv[:, :], dinv[:, :]).then_inc(S["deg_made"], 1)
            dve.wait_ge(S["total_ps"], 1)
            link(v.tensor_copy(n_t[:, :], tmp_ps[0][:, 0:T]))
            link(v.tensor_tensor_scan(end_t[:, :], ones[:, 0:T], n_t[:, :], 0.0, ALU.mult, ALU.add))
            v.tensor_tensor(grp_f[:, 0, :], end_t[:, :], n_t[:, :], ALU.subtract)
            link(v.tensor_scalar(grp_f[:, 1, :], end_t[:, :], -1.0, None, ALU.add))
            dve.wait_ge(S["order_known"], 1)
            with dve.If(dve.value_load(unsorted[0:1, 0:1], min_val=0, max_val=EPAD) > 0):
                dve.wait_ge(S["sort_loaded"], 32)
                dve.wait_ge(S["sort_consts"], 1)
                v.tensor_scalar(sort_tile_i[:, :], sort_dst[:, :], 7, None,
                                ALU.arith_shift_right).then_inc(S["sort_made"], 1)
                dve.wait_ge(S["sort_made"], 1)
                v.tensor_copy(sort_tile[:, :], sort_tile_i[:, :]).then_inc(S["sort_made"], 1)
                dve.wait_ge(S["sort_made"], 2)
                v.tensor_scalar(sort_skip[:, :], sort_tile[:, :], 0.0, float(2 * EPAD), ALU.is_lt,
                                ALU.mult).then_inc(S["sort_done"], 1)
                dve.wait_ge(S["sort_done"], 1)
                with dve.Fori(0, EC) as c:
                    col = bass.ds(c, 1)
                    v.tensor_scalar(sort_oh[:, :], iota_t[:, 0:T], sort_tile[:, col], None,
                                    ALU.is_equal).then_inc(S["sort_oh_made"], 1)
                    v.tensor_copy(edge_val[:, 0:1], sort_src[:, col])
                    v.tensor_copy(edge_val[:, 1:2], sort_dst[:, col])
                    dve.wait_ge(S["sort_ranked"], c + 1)
                    v.tensor_tensor(sort_at[:, 0, :], aggT_ps[:, 0:T], grp_f[:, 0, :],
                                    ALU.add).then_inc(S["sort_read"], 1)
                    dve.wait_ge(S["sort_read"], c * 3 + 1)
                    v.scalar_tensor_tensor(sort_at[:, 1, :], sort_at[:, 0, :], 1.0, sort_oh[:, :], ALU.mult, ALU.mult,
                                           accum_out=place[:, :]).then_inc(S["sort_read"], 1)
                    dve.wait_ge(S["sort_read"], c * 3 + 2)
                    v.tensor_tensor(place_i[:, :], place[:, :], sort_skip[:, col],
                                    ALU.add).then_inc(S["sort_read"], 1)
                    dve.wait_ge(S["sort_read"], c * 3 + 3)
                    dve.sem_inc(S["sort_placed"], 1)
                    dve.wait_ge(S["sort_counted"], c + 1)
                    dve.wait_ge(S["sort_scattered"], (c + 1) * 32)
                dve.sem_inc(S["sort_done"], 1)
            dve.nop()
            link(v.tensor_copy(grp_i[:, :, :], grp_f[:, :, :]))
            link(v.tensor_scalar(grp_s[:, :, :], grp_i[:, :, :], 8, None, ALU.arith_shift_right))
            link(v.tensor_copy(grp_f[:, :, :], grp_s[:, :, :]))
            link(v.tensor_tensor(steps_t[:, :], grp_f[:, 1, :], grp_f[:, 0, :], ALU.subtract))
            link(v.tensor_scalar(steps_t[:, :], steps_t[:, :], 1.0, 1.0, ALU.add, ALU.max))
            link(v.tensor_tensor_scan(send_t[:, :], ones[:, 0:T], steps_t[:, :], 0.0, ALU.mult, ALU.add))
            link(v.tensor_tensor(shift_t[:, :], grp_f[:, 0, :], send_t[:, :], ALU.subtract))
            v.tensor_tensor(shift_t[:, :], shift_t[:, :], steps_t[:, :], ALU.add)
            v.tensor_scalar(win_end[:, :], iota_s[:, 0:1], float(HR), float(HR), ALU.mult, ALU.add)
            link(v.tensor_scalar(next_s[:, :], iota_s[:, :], 1.0, None, ALU.add))
            v.tensor_scalar(pick[:, 2, 0, :], send_t[:, :], win_end[:, :], 0.0, ALU.is_le, ALU.add,
                            accum_out=ended_w[:, :])
            v.tensor_scalar(rooted_w[:, 1:2], next_s[:, 0:1], ROOT_RATE, None, ALU.mult)
            for q in range(SB):
                v.tensor_scalar(pick[:, 0, q, 0:T - 1], send_t[:, 0:T - 1], iota_s[:, q:q + 1], 0.0, ALU.is_le,
                                ALU.add, accum_out=tile_s[:, q:q + 1])
                last = v.scalar_tensor_tensor(pick[:, 1, q, :], send_t[:, :], next_s[:, q:q + 1], iota_t[:, 1:T + 1],
                                              ALU.is_equal, ALU.mult, accum_out=flag_s[:, q:q + 1])
            link(last)
            v.tensor_scalar(rooted_w[:, 0:1], ended_w[:, :], 1.0, rooted_w[:, 1:2], ALU.add, ALU.max)
            for q in range(SB):
                last = v.scalar_tensor_tensor(pick[:, 2, q, :], iota_t[:, 0:T], tile_s[:, q:q + 1], shift_t[:, :],
                                              ALU.is_equal, ALU.mult, accum_out=base_s[:, q:q + 1])
            link(last)
            v.tensor_scalar(rooted_w[:, 0:1], rooted_w[:, 0:1], float(T + 1), None, ALU.min)
            link(v.tensor_tensor(grp_sf[:, :], base_s[:, :], iota_s[:, :], ALU.add))
            link(v.tensor_scalar(grp_sf[:, :], grp_sf[:, :], float(NG), 0.0, ALU.min, ALU.max))
            v.tensor_scalar(tile_s[:, :], tile_s[:, :], float(P), None, ALU.mult)
            v.tensor_copy(grp_si[:, :], grp_sf[:, :]).then_inc(S["sched_ready"], 1)
            dve.wait_ge(S["bias_ps"], 1)
            dve.wait_ge(S["consts_made"], 2)
            split_bias(selfT_ps, bias_hi, bias_lo)
            dve.wait_ge(S["rows_gathered"], 16 * 2 * SB)
            for q in range(SB):
                last = v.tensor_scalar(locf[:, q, :], drow[:, q, :], tile_s[:, q:q + 1], None, ALU.subtract)
            link(last)
            v.tensor_scalar(off_lo[:, :, :], locf[:, :, :], 0.0, SKIP, ALU.is_lt, ALU.mult)
            link(v.tensor_scalar(idxf[:, :, :], locf[:, :, :], float(P - 1), SKIP, ALU.is_gt, ALU.mult))
            link(v.tensor_tensor(idxf[:, :, :], idxf[:, :, :], off_lo[:, :, :], ALU.add))
            link(v.tensor_tensor(idxf[:, :, :], idxf[:, :, :], srow[:, :, :], ALU.add))
            v.tensor_scalar(idxf[:, :, :], idxf[:, :, :], SKIP, None, ALU.min)
            v.tensor_scalar(locf[:, :, :], locf[:, :, :], -1.0, float(P), ALU.max, ALU.min).then_inc(S["tabs_ps"], 1)
            for j in range(CH):
                dve.wait_ge(S["tabs_ps"], 2 + j)
                v.tensor_copy(idx_tab[:, j, :], tmp_ps[0][:, :])
                v.tensor_copy(loc_tab[:, j, :], tmp_ps[1][:, :]).then_inc(S["tabs_read"], 1)
            dve.wait_ge(S["flags_ps"], 1)
            v.tensor_copy(flags[0:1, :], tmp_ps[2][0:1, :])
            v.tensor_copy(rooted[0:1, WPAD:WPAD + P], hist_ps[0:1, P:2 * P])
            v.tensor_copy(ended[0:1, WPAD:WPAD + P], hist_ps[0:1, 0:P]).then_inc(S["tabs_made"], 1)
            dve.wait_ge(S["tabs_made"], 1)
            dve.wait_ge(S["stage_stored0"], 16 * 4)
            dve.wait_ge(S["stage_stored1"], 16 * 3)

            def own_rows(L, r):
                with dve.If(r > 1):
                    prev = nc.s_assert_within(r - 1, 1, T, skip_runtime_bounds_check_because="round 1 is left out")
                    dve.wait_ge(S["root_ready"], r + (T + 1) * (L - 1))
                    if L == 1:
                        v.tensor_copy(tile_of_x(prev), root_ps[:, :]).then_inc(S["root_added"], 1)
                    else:
                        v.tensor_tensor(tile_of_x(prev), root_ps[:, :], tile_of_x(prev),
                                        ALU.add).then_inc(S["root_added"], 1)
                dve.nop()

            def finish(L, t1):
                if L > 0:
                    dve.wait_ge(S["root_added"], t1 + (T * (L - 1) + 1))
                dve.wait_ge(S["prod_ready"], t1 + T * L)
                if L == 1:
                    v.tensor_tensor(tile_of_x(t1), product(t1), tile_of_x(t1), ALU.add).then_inc(S["prod_read"], 1)
                    return
                v.scalar_tensor_tensor(tile_of_x(t1), product(t1), 1.0, tile_of_x(t1), ALU.mult, ALU.add,
                                       accum_out=column(sums, t1)).then_inc(S["prod_read"], 1)
                dve.wait_ge(S["prod_read"], t1 + (T * L + PR))
                v.tensor_scalar(column(sums, t1), column(sums, t1), -1.0 / D, None,
                                ALU.mult).then_inc(S["mean_ready"], 1)
                with dve.If(t1 > NORM_LAG):
                    norm(L, lagged(t1, NORM_LAG))
                dve.nop()

            def norm(L, t1):
                ends = L // 2 * T
                dve.wait_ge(S["root_taken"], t1 + (ends + NORM_LAG))
                v.reciprocal(column(root, t1), column(root, t1)).then_inc(S["rstd_ready"], 1)
                dve.wait_ge(S["rstd_ready"], t1 + (ends + NORM_LAG))
                v.tensor_scalar(tile_of_x(t1), tile_of_x(t1), column(sums, t1), column(root, t1), ALU.add,
                                ALU.mult).then_inc(S["norm_ready"], 1)

            for L in range(NL):
                if L > 0:
                    dve.wait_ge(S["w_loaded"], 16 * (1 + 4 * L))
                    split_bias(agg, aggT, agg)
                if L == 2:
                    dve.wait_ge(S["x_reloaded"], 16 * T)

                def step(b, n):
                    s = b * SLOTS + (NS * L + n + 1)
                    dve.wait_ge(S["gathered"], s)
                    v.tensor_tensor(oh[:, n, :, :], iota_row[:, :].unsqueeze(1).to_broadcast([P, CH, P]),
                                    loc_tab[:, :, bass.ds(b * SLOTS + n, 1)].to_broadcast([P, CH, P]), ALU.is_equal)
                    dve.wait_ge(S["hi_ready"], s)
                    v.tensor_tensor(lo[:, n, :, :], raw[:, n, :, :], hi[:, n, :, :].bitcast(fp32),
                                    ALU.subtract).then_inc(S["lo_ready"], 1)

                def tiles_of(w, part):
                    each(dve, by_end_of(dve, ended, w - 1), by_end_of(dve, ended, w), lambda t1: part(L, t1))

                def own_rounds(w):
                    if L > 0:
                        each(dve, by_end_of(dve, rooted, w - 1), by_end_of(dve, rooted, w),
                             lambda r: own_rows(L, r), T + 1)

                with dve.Fori(0, NS // SLOTS) as b:
                    for n in range(SLOTS):
                        w = b * (SLOTS // HR) + n // HR
                        step(b, n)
                        if n % HR == 1:
                            own_rounds(w - 1)
                        elif n % HR == 3:
                            tiles_of(w - 1, finish)
                own_rounds(NW - 1)
                tiles_of(NW - 1, finish)
                if L != 1:
                    for t1 in range(T - NORM_LAG + 1, T + 1):
                        norm(L, t1)

        @block.scalar
        def _(act):
            a = nc.scalar
            act.sem_inc(S["h_stored"], 16 * (DEV_LAG + 1))
            act.sem_inc(S["h_ready"], DEV_LAG)
            act.sem_inc(S["squares_made"], DEV_LAG)
            act.sem_inc(S["root_taken"], NORM_LAG)
            act.wait_ge(S["consts_made"], 1)
            act.wait_ge(S["deg_made"], 1)
            a.activation(dinv[:, :], dinv[:, :], ACT.Sqrt).then_inc(S["deg_made"], 1)
            act.wait_ge(S["deg_made"], 3)
            act.wait_ge(S["x_loaded"], 16 * (1 + (T - 1) // 8))
            stored = (S["stage_stored0"], S["stage_stored1"])
            for b in range(NB):
                if b >= 2:
                    act.wait_ge(stored[b % 2], 16 * (b // 2))
                for k in range(BT):
                    t = b * BT + k
                    last = a.activation(stage[:, b % 2, k, :], X[:, t, :], ACT.Copy, scale=dinv[:, t:t + 1])
                last.then_inc(S["staged"], 1)
                act.wait_ge(S["staged"], b + 1)
                act.dma_start(tables[0][b * BT * P:(b + 1) * BT * P, :].rearrange("(t p) d -> p t d", p=P),
                              stage[:, b % 2, :, :]).then_inc(stored[b % 2], 16)
            act.wait_ge(S["zeroed"], 1)
            for n in range(NL):
                act.dma_start(tables[n][T * P:(T + 2) * P, :].rearrange("(j p) d -> p j d", p=P),
                              raw[:, 0, :, :]).then_inc(S["zero_stored"], 16)
            act.wait_ge(S["zero_stored"], 16 * NL)
            act.wait_ge(S["tabs_made"], 1)
            act.wait_ge(S["bias_made"], 1)
            act.wait_ge(S["stage_stored0"], 16 * 4)
            act.wait_ge(S["stage_stored1"], 16 * 3)

            def scale_sums(L, t1):
                scale = (dinv, rcnt, rcnt)[L]
                act.wait_ge(S["sum_ready"], t1 + T * L)
                a.activation(agg[:, :], sum_ps[:, :], ACT.Copy,
                             scale=scale[:, bass.ds(t1 - 1, 1)]).then_inc(S["agg_ready"], 1)
                if L == 0:
                    act.dma_start(selfbuf[:, :], tables[L][bass.ds(t1 * P, P), :]).then_inc(S["self_loaded"], 16)
                act.wait_ge(S["aggT_done"], t1 + T * L)
                a.activation(aggT[:, :], aggT_ps[:, :], ACT.Copy).then_inc(S["aggT_ready"], 1)
                with act.If(t1 > DEV_LAG):
                    if L == 1:
                        store(L, lagged(t1, DEV_LAG))
                    else:
                        deviation(L, lagged(t1, DEV_LAG))
                act.nop()
                if L != 1:
                    with act.If(t1 > STORE_LAG):
                        store(L, lagged(t1, STORE_LAG))
                    act.nop()

            def own_rows(L, r):
                act.wait_ge(S["selfT_done"], r + (T + 2) * (L - 1))
                a.activation(selfT[:, :], selfT_ps[:, :], ACT.Copy).then_inc(S["selfT_ready"], 1)
                act.dma_start(selfbuf[:, :], tables[L][bass.ds(r * P, P), :]).then_inc(S["self_loaded"], 16)

            def deviation(L, t1):
                act.wait_ge(S["mean_ready"], t1 + (L // 2 * T + DEV_LAG))
                a.activation(hbuf[:, :], tile_of_x(t1), ACT.Square, bias=column(sums, t1),
                             accum_out=column(sqsum, t1)).then_inc(S["squares_made"], 1)
                act.wait_ge(S["squares_made"], t1 + (L // 2 * T + DEV_LAG))
                a.activation(column(root, t1), column(sqsum, t1), ACT.Sqrt, scale=1.0 / D,
                             bias=eps[:, 0:1]).then_inc(S["root_taken"], 1)

            def store(L, t1):
                if L == 1:
                    act.wait_ge(S["prod_read"], t1 + (T * L + PR))
                    act.wait_ge(S["h_stored"], (t1 + DEV_LAG) * 16)
                    a.activation(hbuf[:, :], tile_of_x(t1), ACT.Relu).then_inc(S["h_ready"], 1)
                    act.wait_ge(S["h_ready"], t1 + DEV_LAG)
                    act.dma_start(tables[2][bass.ds(t1 * P - P, P), :], hbuf[:, :]).then_inc(S["h_stored"], 16)
                    act.dma_start(tile_of_x(t1), tables[1][bass.ds(t1 * P - P, P), :]).then_inc(S["x_reloaded"], 16)
                    return
                act.wait_ge(S["norm_ready"], t1 + (L // 2 * T + STORE_LAG))
                if L == 0:
                    act.dma_start(tables[1][bass.ds(t1 * P - P, P), :], tile_of_x(t1)).then_inc(S["x_stored"], 16)
                else:
                    full = nc.s_assert_within(t1, 1, T - 1, skip_runtime_bounds_check_because="not the last tile")
                    act.dma_start(out[bass.ds(full * P - P, P), :], tile_of_x(full)).then_inc(S["out_stored"], 16)

            for L in range(NL):
                if L == 1:
                    act.wait_ge(S["x_stored"], 16 * T)
                    act.wait_ge(S["self_loaded"], 16 * (T + 1))
                elif L == 2:
                    act.wait_ge(S["h_stored"], 16 * (T + DEV_LAG + 1))
                    act.wait_ge(S["selfT_done"], T + 2)
                act.dma_start(selfbuf[:, :], tables[L][0:P, :]).then_inc(S["self_loaded"], 16)

                def round_rows(base, n):
                    act.wait_ge(S["gathered"], base + (NS * L + n + 1))
                    a.activation(hi[:, n % SLOTS, :, :], raw[:, n % SLOTS, :, :], ACT.Copy).then_inc(S["hi_ready"], 1)

                def sums_of_step(base, n):
                    last_of = act.value_load(flags[0:1, bass.ds(base + n, 1)], min_val=0, max_val=T)
                    with act.If(last_of > 0):
                        scale_sums(L, nc.s_assert_within(last_of, 1, T,
                                                         skip_runtime_bounds_check_because="the flag is not zero"))

                def own_rounds(w):
                    if L > 0:
                        each(act, by_end_of(act, rooted, w - 1), by_end_of(act, rooted, w),
                             lambda r: own_rows(L, r), T + 1)

                def steps(base, w0, final):
                    for n in range(SLOTS):
                        w = w0 + n // HR
                        if not (final and n + LEAD >= SLOTS):
                            round_rows(base, n + LEAD)
                        if n % HR == 0:
                            own_rounds(w - 1)
                        sums_of_step(base, n)

                for n in range(LEAD):
                    round_rows(0, n)
                with act.Fori(0, NS // SLOTS - 1) as b:
                    steps(b * SLOTS, b * (SLOTS // HR), False)
                steps(NS - SLOTS, NW - SLOTS // HR, True)
                own_rounds(NW - 1)
                if L != 1:
                    for t1 in range(T - STORE_LAG + 1, T - NORM_LAG + 1):
                        store(L, t1)
                for t1 in range(T - DEV_LAG + 1, T + 1):
                    (store if L == 1 else deviation)(L, t1)
                if L != 1:
                    for t1 in range(T - NORM_LAG + 1, T + (L == 0)):
                        store(L, t1)
            act.wait_ge(S["norm_ready"], 2 * T + STORE_LAG)
            act.dma_start(out[(T - 1) * P:N, :], X[0:TAIL, T - 1, :]).then_inc(S["out_stored"], 16)
            act.wait_ge(S["out_stored"], 16 * T)
            act.wait_ge(S["self_loaded"], 16 * ((T + 1) + 2 * (T + 2)))

        @block.tensor
        def _(pe):
            mm = nc.tensor.matmul

            def clear(bank, cols):
                return mm(bank[:, 0:cols], zeros[:, :], zeros[:, 0:1].to_broadcast([P, cols]), start=True, stop=False,
                          skip_group_check=True)

            pe.sem_inc(S["oh_used"], 2)
            pe.sem_inc(S["root_added"], 1)
            pe.sem_inc(S["root_ready"], 1)
            pe.sem_inc(S["pe_done"], SLOTS)
            pe.wait_ge(S["consts_made"], 2)
            clear(hist_ps, T)

            def count(b, half):
                pe.wait_ge(S["oh_ready"], b + 1)
                for c in range(HB):
                    last = mm(hist_ps[:, 0:T], oh_lo[:, half, :, c], oh_hi[:, half, :, c], start=False, stop=False,
                              skip_group_check=True)
                last.then_inc(S["oh_used"], 1)

            with pe.Fori(0, EC // HB - 1, 2) as b:
                count(b, 0)
                count(b + 1, 1)
            count(EC // HB - 1, 0)
            pe.wait_ge(S["order_read"], 1)
            mm(aggT_ps[0:1, 0:1], fall_sum[:, :], ones[:, 0:1], start=True, stop=True)
            mm(hist_ps[:, 0:T], zeros[:, :], zeros[:, 0:T], start=False, stop=True,
               skip_group_check=True).then_inc(S["hist_done"], 1)
            pe.wait_ge(S["deg_made"], 1)
            mm(tmp_ps[0][:, 0:T], ones[:, :], cnt[:, :], start=True, stop=True).then_inc(S["total_ps"], 1)
            pe.wait_ge(S["order_known"], 1)
            with pe.If(pe.value_load(unsorted[0:1, 0:1], min_val=0, max_val=EPAD) > 0):
                clear(aggT_ps, T)
                with pe.Fori(0, EC) as c:
                    pe.wait_ge(S["sort_oh_made"], c + 1)
                    mm(aggT_ps[:, 0:T], before[:, :], sort_oh[:, :], start=False, stop=True,
                       skip_group_check=True).then_inc(S["sort_ranked"], 1)
                    pe.wait_ge(S["sort_read"], c * 3 + 1)
                    mm(aggT_ps[:, 0:T], not_before[:, :], sort_oh[:, :], start=False, stop=True,
                       skip_group_check=True).then_inc(S["sort_counted"], 1)
            pe.nop()
            pe.wait_ge(S["loads_done"], 16 * (3 + 2 * KE))
            for k in range(KE):
                mm(selfT_ps[0:2, :], tcol[:, k, :], late_wt[:, k, :], start=(k == 0), stop=False)
            mm(selfT_ps[0:2, :], ones[0:2, 0:2], bin_row[0:2, :], start=False, stop=True).then_inc(S["bias_ps"], 1)
            pe.wait_ge(S["bias_made"], 1)
            pe.wait_ge(S["tabs_ps"], 1)
            for q in range(SB):
                nc.tensor.transpose(tmp_ps[2][0:1, q * P:(q + 1) * P], flag_s[:, q:q + 1], ident[:, :])
            nc.tensor.transpose(hist_ps[0:1, 0:P], ended_w[:, :], ident[:, :])
            last = nc.tensor.transpose(hist_ps[0:1, P:2 * P], rooted_w[:, 0:1], ident[:, :])
            last.then_inc(S["flags_ps"], 1)
            for j in range(CH):
                if j > 0:
                    pe.wait_ge(S["tabs_read"], j)
                for q in range(SB):
                    nc.tensor.transpose(tmp_ps[0][:, q * P:(q + 1) * P], idxf[:, q, j * P:(j + 1) * P], ident[:, :])
                for q in range(SB):
                    last = nc.tensor.transpose(tmp_ps[1][:, q * P:(q + 1) * P], locf[:, q, j * P:(j + 1) * P],
                                               ident[:, :])
                last.then_inc(S["tabs_ps"], 1)
            pe.wait_ge(S["tabs_made"], 1)

            def take_sums(L, t1):
                tile = t1 + T * L
                if L == 0:
                    pe.wait_ge(S["self_loaded"], t1 * 16)
                    mm(sum_ps[:, :], ident[:, :], selfbuf[:, :], start=False, stop=True,
                       skip_group_check=True).then_inc(S["sum_ready"], 1)
                else:
                    mm(sum_ps[:, 0:1], zeros[:, :], zeros[:, 0:1], start=False, stop=True,
                       skip_group_check=True).then_inc(S["sum_ready"], 1)
                pe.wait_ge(S["agg_ready"], tile)
                for k in range(KD):
                    last = nc.tensor.transpose(aggT_ps[:, k * P:(k + 1) * P], agg[:, k * P:(k + 1) * P], ident[:, :])
                last.then_inc(S["aggT_done"], 1)
                clear(sum_ps, D)
                pe.wait_ge(S["prod_read"], tile)
                if L == 0:
                    mm(product(t1), ones[0:2, :].bitcast(f32r), brow[0:2, :], start=True, stop=False)
                pe.wait_ge(S["aggT_ready"], tile)
                by_weights(product(t1), aggT, 0, S["prod_ready"], L > 0)

            def by_weights(out_ps, xT, n, done, open_bank):
                for k in range(KD):
                    last = mm(out_ps, xT[:, k * P:(k + 1) * P], W[:, n, k, :], start=(open_bank and k == 0),
                              stop=(k == KD - 1))
                last.then_inc(done, 1)

            def own_rows(L, r):
                pe.wait_ge(S["root_added"], r + T * (L - 1))
                pe.wait_ge(S["selfT_ready"], r + (T + 1) * (L - 1))
                mm(root_ps[:, :], ones[0:2, :].bitcast(f32r), brow[0:2, :], start=True, stop=False)
                by_weights(root_ps[:, :], selfT, 1, S["root_ready"], False)
                pe.wait_ge(S["self_loaded"], (r + (T + 1 + (T + 2) * (L - 1) + 1)) * 16)
                transpose_own()

            def transpose_own():
                for k in range(KD):
                    last = nc.tensor.transpose(selfT_ps[:, k * P:(k + 1) * P], selfbuf[:, k * P:(k + 1) * P],
                                               ident[:, :])
                last.then_inc(S["selfT_done"], 1)

            clear(sum_ps, D)
            for L in range(NL):
                pe.wait_ge(S["w_loaded"], 16 * (1 + 4 * L))
                pe.wait_ge(S["bias_made"], L + 1)
                if L > 0:
                    pe.wait_ge(S["self_loaded"], (T + 1 + (T + 2) * (L - 1) + 1) * 16)
                    transpose_own()

                def window_parts(w):
                    if L > 0:
                        each(pe, by_end_of(pe, rooted, w - 2), by_end_of(pe, rooted, w - 1),
                             lambda r: own_rows(L, r), T + 1)

                with pe.Fori(0, NS // SLOTS) as b:
                    for n in range(SLOTS):
                        last_of = pe.value_load(flags[0:1, bass.ds(b * SLOTS + n, 1)], min_val=0, max_val=T)
                        pe.wait_ge(S["lo_ready"], b * SLOTS + (NS * L + n + 1))
                        for half in (hi[:, n, :, :], lo[:, n, :, :]):
                            for j in range(CH):
                                last = mm(sum_ps[:, :], oh[:, n, j, :], half[:, j, :], start=False, stop=False,
                                          skip_group_check=True)
                        last.then_inc(S["pe_done"], 1)
                        if n % HR == 0:
                            window_parts(b * (SLOTS // HR) + n // HR)
                        with pe.If(last_of > 0):
                            take_sums(L, nc.s_assert_within(last_of, 1, T,
                                                            skip_runtime_bounds_check_because="the flag is not zero"))
                window_parts(NW)


_INS = ['x', 'src', 'dst', 'L0_gnn_t_emb', 'L0_gnn_W', 'L0_gnn_b', 'L0_gnn_Wt', 'L0_gnn_bt', 'L1_gnn_Wl1', 'L1_gnn_Wr1',
        'L1_gnn_b1', 'L1_gnn_Wl2', 'L1_gnn_Wr2', 'L1_gnn_b2']
_TRANSPOSED = ('L1_gnn_Wl1', 'L1_gnn_Wr1', 'L1_gnn_Wl2', 'L1_gnn_Wr2')


def build(nc, arrays):
    args = [nc.dram_tensor(f"in_{n}", arrays[f"in_{n}"].shape, mybir.dt.from_np(arrays[f"in_{n}"].dtype),
                           kind="ExternalInput").ap() for n in _INS]
    out = nc.dram_tensor("out_0", arrays["in_x"].shape, mybir.dt.float32, kind="ExternalOutput").ap()
    gnn_resnorm(nc, *args, out)


def kernel(**inputs):
    import numpy as np
    import concourse.bacc as bacc
    from concourse.bass_utils import run_bass_kernel_spmd

    nc = bacc.Bacc("TRN2", target_bir_lowering=False, num_devices=1)
    arrays = {}
    for n in _INS:
        w = np.asarray(inputs[n])
        arrays[f"in_{n}"] = np.ascontiguousarray(w.T if n in _TRANSPOSED else w)
    build(nc, arrays)
    return run_bass_kernel_spmd(nc, [arrays], core_ids=[0]).results[0]["out_0"]
```
